# Optimizing a Trainium2 kernel written in Bass

```python
import numpy as np
import jax
import jax.numpy as jnp

def _softmax(x, axis=-1):
    return jax.nn.softmax(x, axis=axis)

def _gelu(x):
    return jax.nn.gelu(x, approximate=True)

def _silu(x):
    return jax.nn.silu(x)

def _sigmoid(x):
    return jax.nn.sigmoid(x)

def _layernorm(x, axis=-1, eps=1e-05):
    m = jnp.mean(x, axis=axis, keepdims=True)
    v = jnp.var(x, axis=axis, keepdims=True)
    return (x - m) / jnp.sqrt(v + eps)

def _scatter_add(tgt, idx, src, axis=0):
    return tgt.at[idx].add(src)

def _segment_sum(src, seg, n):
    return jax.ops.segment_sum(src, seg, n)
kernel_name = 'mk_seq_preln_d1_jaxref_r8_41916b'

def setup_inputs(seed: int=0):
    np.random.seed(seed)
    _w = jnp.asarray

    def _L0_attn_setup():
        import jax, jax.numpy as jnp
        from jax import lax
        import numpy as np
        D_MODEL, D_INNER, D_STATE, D_CONV, DT_RANK, HIDDEN = (256, 512, 16, 4, 128, 1024)
        B, L = (2, 256)

        def _layernorm(x, w, b, eps=1e-05):
            m = x.mean(-1, keepdims=True)
            v = x.var(-1, keepdims=True)
            return (x - m) / jnp.sqrt(v + eps) * w + b

        def _mamba(u, in_proj_w, conv_w, conv_b, x_proj_w, dt_proj_w, dt_proj_b, A_log, D_skip, out_proj_w):
            d_inner, d_state = A_log.shape
            d_conv = conv_w.shape[-1]
            dt_rank = dt_proj_w.shape[1]
            xz = u @ in_proj_w.T
            xm, z = jnp.split(xz, 2, axis=-1)
            xc = lax.conv_general_dilated(jnp.transpose(xm, (0, 2, 1)), conv_w, (1,), [(d_conv - 1, 0)], dimension_numbers=('NCH', 'OIH', 'NCH'), feature_group_count=d_inner)
            xc = jax.nn.silu(xc + conv_b[None, :, None])
            xc = jnp.transpose(xc, (0, 2, 1))
            x_dbl = xc @ x_proj_w.T
            dt, Bm, Cm = jnp.split(x_dbl, [dt_rank, dt_rank + d_state], axis=-1)
            dt = jax.nn.softplus(dt @ dt_proj_w.T + dt_proj_b)
            A = -jnp.exp(A_log)

            def step(h, t):
                dt_t, B_t, C_t, x_t = t
                dA = jnp.exp(dt_t[..., None] * A)
                h = h * dA + dt_t[..., None] * B_t[:, None, :] * x_t[..., None]
                y = jnp.einsum('bds,bs->bd', h, C_t)
                return (h, y)
            h0 = jnp.zeros((u.shape[0], d_inner, d_state), dtype=u.dtype)
            xs = (jnp.swapaxes(dt, 0, 1), jnp.swapaxes(Bm, 0, 1), jnp.swapaxes(Cm, 0, 1), jnp.swapaxes(xc, 0, 1))
            _, ys = lax.scan(step, h0, xs)
            y = jnp.swapaxes(ys, 0, 1) + xc * D_skip
            y = y * jax.nn.silu(z)
            return y @ out_proj_w.T
        key = jax.random.key(seed)
        ks = jax.random.split(key, 12)
        s = 0.02
        f32 = jnp.float32
        A_init = jnp.broadcast_to(jnp.arange(1, D_STATE + 1, dtype=f32), (D_INNER, D_STATE))
        return {'x': jax.random.normal(ks[0], (B, L, D_MODEL), f32), 'ln1_w': jnp.ones((D_MODEL,), f32), 'ln1_b': jnp.zeros((D_MODEL,), f32), 'ln2_w': jnp.ones((D_MODEL,), f32), 'ln2_b': jnp.zeros((D_MODEL,), f32), 'in_proj_w': jax.random.normal(ks[1], (2 * D_INNER, D_MODEL), f32) * s, 'conv_w': jax.random.normal(ks[2], (D_INNER, 1, D_CONV), f32) * 0.2, 'conv_b': jnp.zeros((D_INNER,), f32), 'x_proj_w': jax.random.normal(ks[3], (DT_RANK + 2 * D_STATE, D_INNER), f32) * s, 'dt_proj_w': jax.random.normal(ks[4], (D_INNER, DT_RANK), f32) * DT_RANK ** (-0.5), 'dt_proj_b': jnp.log(jnp.expm1(jnp.exp(jax.random.uniform(ks[5], (D_INNER,), f32, np.log(0.001), np.log(0.1))))), 'A_log': jnp.log(A_init), 'D_skip': jnp.ones((D_INNER,), f32), 'out_proj_w': jax.random.normal(ks[6], (D_MODEL, D_INNER), f32) * s, 'ff_proj_w': jax.random.normal(ks[7], (HIDDEN, D_MODEL), f32) * s, 'ff_out_w': jax.random.normal(ks[8], (D_MODEL, HIDDEN // 2), f32) * s}
    _L0_attn_in = _L0_attn_setup()

    def _L0_ffn_setup():
        import jax, jax.numpy as jnp
        import numpy as np
        IN_F, OUT_F = (256, 256)
        N_EXPERTS, RANK, TOP_K = (8, 128, 2)
        key = jax.random.key(seed)
        k_x, k_r, k_a, k_b = jax.random.split(key, 4)
        hidden_states = jax.random.normal(k_x, (4, 512, IN_F), dtype=jnp.float32)
        router_w = jax.random.normal(k_r, (IN_F, N_EXPERTS), dtype=jnp.float32) * IN_F ** (-0.5)
        Wa = jax.random.normal(k_a, (N_EXPERTS, IN_F, RANK), dtype=jnp.float32) * IN_F ** (-0.5)
        Wb = jax.random.normal(k_b, (N_EXPERTS, RANK, OUT_F), dtype=jnp.float32) * RANK ** (-0.5)
        return {'hidden_states': hidden_states, 'router_w': router_w, 'Wa': Wa, 'Wb': Wb}
    _L0_ffn_in = _L0_ffn_setup()
    _d = {'L0_attn_x': _L0_attn_in['x'], 'L0_attn_ln1_w': _L0_attn_in['ln1_w'], 'L0_attn_ln1_b': _L0_attn_in['ln1_b'], 'L0_attn_ln2_w': _L0_attn_in['ln2_w'], 'L0_attn_ln2_b': _L0_attn_in['ln2_b'], 'L0_attn_in_proj_w': _L0_attn_in['in_proj_w'], 'L0_attn_conv_w': _L0_attn_in['conv_w'], 'L0_attn_conv_b': _L0_attn_in['conv_b'], 'L0_attn_x_proj_w': _L0_attn_in['x_proj_w'], 'L0_attn_dt_proj_w': _L0_attn_in['dt_proj_w'], 'L0_attn_dt_proj_b': _L0_attn_in['dt_proj_b'], 'L0_attn_A_log': _L0_attn_in['A_log'], 'L0_attn_D_skip': _L0_attn_in['D_skip'], 'L0_attn_out_proj_w': _L0_attn_in['out_proj_w'], 'L0_attn_ff_proj_w': _L0_attn_in['ff_proj_w'], 'L0_attn_ff_out_w': _L0_attn_in['ff_out_w'], 'L0_ffn_router_w': _L0_ffn_in['router_w'], 'L0_ffn_Wa': _L0_ffn_in['Wa'], 'L0_ffn_Wb': _L0_ffn_in['Wb']}
    _x0 = _d['L0_attn_x']
    _d['L0_attn_x'] = jax.random.normal(jax.random.fold_in(jax.random.key(seed), 1), (2, 2048, 256), dtype=_x0.dtype)
    del _x0
    return _d

def reference(L0_attn_x, L0_attn_ln1_w, L0_attn_ln1_b, L0_attn_ln2_w, L0_attn_ln2_b, L0_attn_in_proj_w, L0_attn_conv_w, L0_attn_conv_b, L0_attn_x_proj_w, L0_attn_dt_proj_w, L0_attn_dt_proj_b, L0_attn_A_log, L0_attn_D_skip, L0_attn_out_proj_w, L0_attn_ff_proj_w, L0_attn_ff_out_w, L0_ffn_router_w, L0_ffn_Wa, L0_ffn_Wb):

    def _L0_attn_ref(x, ln1_w, ln1_b, ln2_w, ln2_b, in_proj_w, conv_w, conv_b, x_proj_w, dt_proj_w, dt_proj_b, A_log, D_skip, out_proj_w, ff_proj_w, ff_out_w):
        import jax, jax.numpy as jnp
        from jax import lax
        import numpy as np
        D_MODEL, D_INNER, D_STATE, D_CONV, DT_RANK, HIDDEN = (256, 512, 16, 4, 128, 1024)
        B, L = (2, 256)

        def _layernorm(x, w, b, eps=1e-05):
            m = x.mean(-1, keepdims=True)
            v = x.var(-1, keepdims=True)
            return (x - m) / jnp.sqrt(v + eps) * w + b

        def _mamba(u, in_proj_w, conv_w, conv_b, x_proj_w, dt_proj_w, dt_proj_b, A_log, D_skip, out_proj_w):
            d_inner, d_state = A_log.shape
            d_conv = conv_w.shape[-1]
            dt_rank = dt_proj_w.shape[1]
            xz = u @ in_proj_w.T
            xm, z = jnp.split(xz, 2, axis=-1)
            xc = lax.conv_general_dilated(jnp.transpose(xm, (0, 2, 1)), conv_w, (1,), [(d_conv - 1, 0)], dimension_numbers=('NCH', 'OIH', 'NCH'), feature_group_count=d_inner)
            xc = jax.nn.silu(xc + conv_b[None, :, None])
            xc = jnp.transpose(xc, (0, 2, 1))
            x_dbl = xc @ x_proj_w.T
            dt, Bm, Cm = jnp.split(x_dbl, [dt_rank, dt_rank + d_state], axis=-1)
            dt = jax.nn.softplus(dt @ dt_proj_w.T + dt_proj_b)
            A = -jnp.exp(A_log)

            def step(h, t):
                dt_t, B_t, C_t, x_t = t
                dA = jnp.exp(dt_t[..., None] * A)
                h = h * dA + dt_t[..., None] * B_t[:, None, :] * x_t[..., None]
                y = jnp.einsum('bds,bs->bd', h, C_t)
                return (h, y)
            h0 = jnp.zeros((u.shape[0], d_inner, d_state), dtype=u.dtype)
            xs = (jnp.swapaxes(dt, 0, 1), jnp.swapaxes(Bm, 0, 1), jnp.swapaxes(Cm, 0, 1), jnp.swapaxes(xc, 0, 1))
            _, ys = lax.scan(step, h0, xs)
            y = jnp.swapaxes(ys, 0, 1) + xc * D_skip
            y = y * jax.nn.silu(z)
            return y @ out_proj_w.T
        mix = _mamba(_layernorm(x, ln1_w, ln1_b), in_proj_w, conv_w, conv_b, x_proj_w, dt_proj_w, dt_proj_b, A_log, D_skip, out_proj_w)
        x = x + mix
        og = x
        h = _layernorm(x, ln2_w, ln2_b) @ ff_proj_w.T
        a, gate = jnp.split(h, 2, axis=-1)
        h = jax.nn.silu(gate) * a
        return og + h @ ff_out_w.T

    def _L0_ffn_ref(hidden_states, router_w, Wa, Wb):
        import jax, jax.numpy as jnp
        import numpy as np
        IN_F, OUT_F = (256, 256)
        N_EXPERTS, RANK, TOP_K = (8, 128, 2)
        B, S, D = hidden_states.shape
        x = hidden_states.reshape(-1, D)
        norm = jnp.maximum(jnp.linalg.norm(x, axis=-1, keepdims=True), 1e-12)
        router_logits = x / norm @ router_w
        routing_weights = jax.nn.softmax(router_logits.astype(jnp.float32), axis=-1)
        rw, selected_experts = jax.lax.top_k(routing_weights, TOP_K)
        rw = rw / jnp.sum(rw, axis=-1, keepdims=True)
        rw = rw.astype(hidden_states.dtype)
        combine = jnp.sum(jax.nn.one_hot(selected_experts, N_EXPERTS, dtype=rw.dtype) * rw[..., None], axis=1)
        out = jnp.zeros((x.shape[0], OUT_F), dtype=hidden_states.dtype)
        for e in range(N_EXPERTS):
            out = out + combine[:, e, None] * (x @ Wa[e] @ Wb[e])
        return out.reshape(B, S, OUT_F)
    x = L0_attn_x
    x = x + _L0_attn_ref(_layernorm(x, axis=-1), L0_attn_ln1_w, L0_attn_ln1_b, L0_attn_ln2_w, L0_attn_ln2_b, L0_attn_in_proj_w, L0_attn_conv_w, L0_attn_conv_b, L0_attn_x_proj_w, L0_attn_dt_proj_w, L0_attn_dt_proj_b, L0_attn_A_log, L0_attn_D_skip, L0_attn_out_proj_w, L0_attn_ff_proj_w, L0_attn_ff_out_w)
    x = x + _L0_ffn_ref(_layernorm(x, axis=-1), L0_ffn_router_w, L0_ffn_Wa, L0_ffn_Wb)
    return x

_drawn_inputs = setup_inputs


def setup_inputs(seed=0):
    import zlib

    import numpy as np

    out = dict(_drawn_inputs(seed))
    spreads = {'L0_attn_ln1_w': (1.0, 0.6),
     'L0_attn_ln1_b': (0.0, 0.8),
     'L0_attn_ln2_w': (1.0, 0.568),
     'L0_attn_ln2_b': (0.0, 0.511),
     'L0_attn_conv_b': (0.0, 0.413),
     'L0_attn_D_skip': (1.0, 0.6)}
    factors = {'L0_attn_conv_w': 2.961,
     'L0_attn_x_proj_w': 8.0,
     'L0_attn_dt_proj_w': 8.0,
     'L0_attn_dt_proj_b': 8.0,
     'L0_attn_A_log': 8.0}
    for name, (base, spread) in spreads.items():
        noise = np.random.default_rng([zlib.crc32(name.encode()), seed]).standard_normal(out[name].shape)
        drawn = base * np.exp(spread * noise) if base else spread * noise
        out[name] = jnp.asarray(drawn.astype(out[name].dtype))
    for name, factor in factors.items():
        out[name] = (out[name] * factor).astype(out[name].dtype)
    return out
```

```python
import math
from contextlib import ExitStack

import concourse.bass as bass
from concourse import mybir

B, L, DM, DI, S, TAPS, DTR, HID = 2, 2048, 256, 512, 16, 4, 128, 1024
NE, RANK = 8, 128
P = 128
T = 256
SUB = T // P
KM = DM // P
NJ = DI // P
NC = L // T
G = 4
NG = S // G
RINGG = 2
RB = 2
F1 = HID // 2 // P
EPS = 1e-5
NORM_FLOOR = 1e-12
LIFT = 20

C_CONVW, C_CONVB, C_DTB, C_DSKIP, C_ALOG = 0, NJ * TAPS, NJ * TAPS + NJ, NJ * TAPS + 2 * NJ, NJ * TAPS + 3 * NJ
C_LN1W = C_ALOG + NJ * S
C_LN1B, C_LN2W, C_LN2B = C_LN1W + KM, C_LN1W + 2 * KM, C_LN1W + 3 * KM
NPAR = C_LN1W + 4 * KM

FRONT_UNITS = ["uT", "z0", "z1", "x0", "x1", "low", "dt0", "dt1"]
BACK_UNITS = ["op", "vT", "ff0", "ff1", "ff2", "ff3", "fo", "xeT", "rt", "cT", "wa0", "wa1", "wa2", "wa3", "wb"]
RING = 3

LINKS_FRONT = 2 + 1
LINKS_BACK = 2 + 2 + 9


def count(per_step, step, k):
    c, b = step
    value = c * (2 * per_step) + (per_step * b + k)
    return max(value, 0) if isinstance(value, int) else value


def is_first(step):
    return isinstance(step[0], int) and step == (0, 0)


def drive(eng, front, main, back):
    def step(before, now, after):
        for s in range(S):
            if before:
                back(s, before)
            if after:
                front(s, after)
            if now:
                main(s, now)

    step(None, None, (0, 0))
    step(None, (0, 0), (0, 1))
    step((0, 0), (0, 1), (1, 0))
    with eng.Fori(1, NC - 1) as c:
        step((c - 1, 1), (c, 0), (c, 1))
        step((c, 0), (c, 1), (c + 1, 0))
    step((NC - 2, 1), (NC - 1, 0), (NC - 1, 1))
    step((NC - 1, 0), (NC - 1, 1), None)
    step((NC - 1, 1), None, None)


def mamba_moe(nc, x, params, w_in, w_x, w_dt, w_out, w_ff, w_fo, w_a, w_b, w_r, bc_scratch, cw_scratch, out):
    f32 = mybir.dt.float32
    ALU = mybir.AluOpType
    ACT = mybir.ActivationFunctionType
    X = mybir.AxisListType.X

    x_v = x.rearrange("b (c j p) d -> c b p j d", p=P, j=SUB)
    out_v = out.rearrange("b (c j p) d -> c b p j d", p=P, j=SUB)

    ctx = ExitStack()
    with ctx:
        def sb(name, shape):
            return ctx.enter_context(nc.sbuf_tensor(name, shape, f32))

        def sem(name):
            return ctx.enter_context(nc.semaphore(name))

        par = sb("par", [P, NPAR])
        w_in_sb = sb("w_in_sb", [P, KM, 2 * DI])
        w_x_sb = sb("w_x_sb", [P, NJ, DTR + 2 * S])
        w_dt_sb = sb("w_dt_sb", [P, DI])
        w_out_sb = sb("w_out_sb", [P, NJ, DM])
        w_ff_sb = sb("w_ff_sb", [P, KM, HID])
        w_fo_sb = sb("w_fo_sb", [P, F1, DM])
        w_a_sb = sb("w_a_sb", [P, KM, NE * RANK])
        w_b_sb = sb("w_b_sb", [P, NE, DM])
        w_r_sb = sb("w_r_sb", [P, KM, NE])
        ident = sb("ident", [P, P])
        earlier = sb("earlier", [P, NE, NE])
        neg_a = sb("neg_a", [P, NJ, S])
        exp_a = sb("exp_a", [P, NJ, S])
        eps_c = sb("eps_c", [P, 1])
        lift_c = sb("lift_c", [P, 1])

        xf = sb("xf", [P, SUB, DM])
        xn = sb("xn", [P, B, SUB, DM])
        un = sb("un", [P, SUB, DM])
        uT = sb("uT", [P, KM, T])
        xm = sb("xm", [P, B, NJ, TAPS - 1 + T])
        acc = sb("acc", [P, NJ, T])
        xc = sb("xc", [P, B, NJ, T])
        sz = sb("sz", [P, B, NJ, T])
        low = sb("low", [P, T])
        bc = sb("bc", [2 * S, T])
        sp_e = sb("sp_e", [P, NJ, T])
        sp_l = sb("sp_l", [P, NJ, T])
        dt = sb("dt", [P, B, NJ, T])
        u = sb("u", [P, B, NJ, T])
        bn = [sb(f"bn{k}", [P, SUB, 6]) for k in range(4)]
        mv = [sb(f"mv{k}", [P, SUB, 2]) for k in range(4)]
        lnv = [sb(f"lnv{k}", [P, SUB]) for k in range(4)]
        rstd = [sb(f"rstd{k}", [P, SUB]) for k in range(4)]

        pause = sb("pause", [P, 1])

        bB = sb("bB", [P, RINGG, G, T])
        bC = sb("bC", [P, RINGG, G, T])
        dA = sb("dA", [P, RB, NJ, T])
        bx = sb("bx", [P, RB, NJ, T])
        h = sb("h", [P, RB, NJ, T])
        hC = sb("hC", [P, RB, NJ, T])
        state = sb("state", [P, B, NJ, S])

        xb = sb("xb", [P, SUB, DM])
        yg = sb("yg", [P, NJ, T])
        x1 = sb("x1", [P, SUB, DM])
        x1x = sb("x1x", [P, SUB, DM])
        vn = sb("vn", [P, SUB, DM])
        vT = sb("vT", [P, KM, T])
        gate = sb("gate", [P, 2, T])
        hg = sb("hg", [P, F1, T])
        x2 = sb("x2", [P, SUB, DM])
        xe = sb("xe", [P, SUB, DM])
        xeT = sb("xeT", [P, KM, T])
        nrm = sb("nrm", [P, 3, SUB])
        lnn = sb("lnn", [P, SUB])
        rn = sb("rn", [P, SUB])
        lg = sb("lg", [P, SUB, NE])
        lgm = sb("lgm", [P, SUB, NE])
        mx = sb("mx", [P, SUB])
        pr = sb("pr", [P, SUB, NE])
        gt = sb("gt", [P, SUB, NE, NE])
        eq = sb("eq", [P, SUB, NE, NE])
        rank = sb("rank", [P, SUB, NE])
        psel = sb("psel", [P, SUB, NE])
        den = sb("den", [P, SUB])
        rden = sb("rden", [P, SUB])
        cw = sb("cw", [P, SUB, NE])
        cT = sb("cT", [NE, T])
        cbc = sb("cbc", [P, NE, T])
        hE = sb("hE", [P, NE, T])
        fin = sb("fin", [P, SUB, DM])

        psy = [ctx.enter_context(nc.psum_tensor(f"psy{i}", [P, 2, T], f32)) for i in range(2)]
        psf = [ctx.enter_context(nc.psum_tensor(f"psf{i}", [P, 2, T], f32)) for i in range(RING)]
        psb = [ctx.enter_context(nc.psum_tensor(f"psb{i}", [P, 2, T], f32)) for i in range(RING)]

        loaded = {k: sem(f"loaded_{k}") for k in ("par", "in", "x", "dt", "out", "ff", "fo", "a", "b", "r")}
        ident_zero, ident_ready = sem("ident_zero"), sem("ident_ready")
        earlier_one, earlier_ready = sem("earlier_one"), sem("earlier_ready")
        consts_ready, state_zero, halo_zero = sem("consts_ready"), sem("state_zero"), sem("halo_zero")
        a_exp, a_ready = sem("a_exp"), sem("a_ready")
        filled_f, filled_b = sem("filled_f"), sem("filled_b")
        xf_loaded, xb_loaded = sem("xf_loaded"), sem("xb_loaded")
        stats = [sem(f"stats{k}") for k in range(4)]
        lnv_done = [sem(f"lnv_done{k}") for k in range(4)]
        rstd_done = [sem(f"rstd_done{k}") for k in range(4)]
        xn_done, un_done, uT_done = sem("xn_done"), sem("un_done"), sem("uT_done")
        halo_moved, xm_done, conv_tap = sem("halo_moved"), sem("xm_done"), sem("conv_tap")
        sz_done, xc_done = sem("sz_done"), sem("xc_done")
        low_done, bc_done = sem("low_done"), sem("bc_done")
        bc_stored = sem("bc_stored")
        b_loaded = [sem(f"b_loaded{i}") for i in range(RINGG)]
        c_loaded = [sem(f"c_loaded{i}") for i in range(RINGG)]
        relu_done, sp_exp, sp_ln = sem("relu_done"), sem("sp_exp"), sem("sp_ln")
        sp_one, sp_masked = sem("sp_one"), sem("sp_masked")
        sp_back, sp_rest, sp_log = sem("sp_back"), sem("sp_rest"), sem("sp_log")
        dt_done, u_done = sem("dt_done"), sem("u_done")
        exp_done, bx_done, scan_done = sem("exp_done"), sem("bx_done"), sem("scan_done")
        hc_done, state_saved, y_summed = sem("hc_done"), sem("state_saved"), sem("y_summed")
        y_skip, yg_done = sem("y_skip"), sem("yg_done")
        x1_done, x1x_done = sem("x1_done"), sem("x1x_done")
        vn_done, vT_done = sem("vn_done"), sem("vT_done")
        gate_done, hg_done = sem("gate_done"), sem("hg_done")
        x2_done, xe_done, xeT_done = sem("x2_done"), sem("xe_done"), sem("xeT_done")
        nrm_done, lnn_done, rn_done = sem("nrm_done"), sem("lnn_done"), sem("rn_done")
        lgm_done, pr_done, cw_done, cT_done = sem("lgm_done"), sem("pr_done"), sem("cw_done"), sem("cT_done")
        cw_stored, cbc_loaded = sem("cw_stored"), sem("cbc_loaded")
        hE_done, fin_done, out_stored = sem("hE_done"), sem("fin_done"), sem("out_stored")
        front_chain, back_chain = sem("front_chain"), sem("back_chain")

        def pcol(col):
            return par[:, col:col + 1]

        def front_bank(name):
            return psf[FRONT_UNITS.index(name) % RING]

        def back_bank(name):
            return psb[BACK_UNITS.index(name) % RING]

        def front_use(name, m):
            return count(len(FRONT_UNITS), m, FRONT_UNITS.index(name) + 1)

        def back_use(name, m):
            return count(len(BACK_UNITS), m, BACK_UNITS.index(name) + 1)

        def front_use_before(name, m):
            return count(len(FRONT_UNITS), m, FRONT_UNITS.index(name) + 1 - len(FRONT_UNITS))

        def back_use_before(name, m):
            return count(len(BACK_UNITS), m, BACK_UNITS.index(name) + 1 - len(BACK_UNITS))

        block = ctx.enter_context(nc.Block())

        @block.sync
        def _(sp):
            def flat(w):
                return w[:, :, :].rearrange("p k m -> p (k m)") if len(w.shape) == 3 else w[:, :]

            sp.dma_start(par[:, :], params).then_inc(loaded["par"], 16)

            for key, dst, src in (("in", w_in_sb, w_in), ("x", w_x_sb, w_x), ("dt", w_dt_sb, w_dt)):
                sp.dma_start(flat(dst), src).then_inc(loaded[key], 16)
            late = [("out", w_out_sb, w_out), ("ff", w_ff_sb, w_ff), ("fo", w_fo_sb, w_fo), ("r", w_r_sb, w_r),
                    ("a", w_a_sb, w_a), ("b", w_b_sb, w_b)]

            def value(v):
                if not isinstance(v, int):
                    sp.compute_val(v)
                return v

            def load_group(m, g, read=None):
                if read is None:
                    read = value(count(S, m, G * (g - RINGG + 1)))
                sp.wait_ge(bx_done, read)
                sp.dma_start(bB[:, g % RINGG], bc_scratch[g * G:(g + 1) * G, :].partition_broadcast(P)
                             ).then_inc(b_loaded[g % RINGG], 16)
                sp.wait_ge(hc_done, read)
                sp.dma_start(bC[:, g % RINGG], bc_scratch[S + g * G:S + (g + 1) * G, :].partition_broadcast(P)
                             ).then_inc(c_loaded[g % RINGG], 16)

            def front(s, m):
                if s == 10:
                    spread, read = value(count(16 * NG // RINGG, m, 0)), value(count(1, m, 1))
                    for i in range(RINGG):
                        sp.wait_ge(b_loaded[i], spread)
                        sp.wait_ge(c_loaded[i], spread)
                    sp.wait_ge(bc_done, read)
                    sp.dma_start(bc_scratch, bc[:, :]).then_inc(bc_stored, 16)
                if s == 13:
                    stored, read = value(count(16, m, 16)), value(count(S, m, -G))
                    sp.wait_ge(bc_stored, stored)
                    load_group(m, 0, read)
                if s == 15 and is_first(m):
                    for key, dst, src in late:
                        sp.dma_start(flat(dst), src).then_inc(loaded[key], 16)

            def main(s, n):
                if s in (0, 4, 8):
                    load_group(n, 1 + s // 4)

            def back(s, m):
                if s == 10:
                    before, ready = value(count(16, m, 0)), value(count(1, m, 1))
                    stored, used = value(count(16, m, 16)), value(count(NE // 2, m, 0))
                    sp.wait_ge(cbc_loaded, before)
                    sp.wait_ge(cT_done, ready)
                    sp.dma_start(cw_scratch, cT[:, :]).then_inc(cw_stored, 16)
                    sp.wait_ge(cw_stored, stored)
                    sp.wait_ge(hE_done, used)
                    sp.dma_start(cbc[:, :, :], cw_scratch.partition_broadcast(P)).then_inc(cbc_loaded, 16)
                if s == 15:
                    sp.wait_ge(fin_done, count(1, m, 1))
                    sp.dma_start(out_v[m[0], m[1]], fin[:, :, :]).then_inc(out_stored, 16)

            drive(sp, front, main, back)
            sp.wait_ge(out_stored, 16 * B * NC)

        @block.gpsimd
        def _(pool):
            nc.gpsimd.memset(ident[:, :], 0.0).then_inc(ident_zero, 1)
            pool.wait_ge(ident_zero, 1)
            nc.gpsimd.affine_select(out=ident[:, :], in_=ident[:, :], compare_op=ALU.not_equal, fill=1.0,
                                    base=0, pattern=[[-1, P]], channel_multiplier=1).then_inc(ident_ready, 1)
            nc.gpsimd.memset(earlier[:, :, :], 1.0).then_inc(earlier_one, 1)
            pool.wait_ge(earlier_one, 1)
            nc.gpsimd.affine_select(out=earlier[:, :, :], in_=earlier[:, :, :], compare_op=ALU.is_gt, fill=0.0,
                                    base=0, pattern=[[1, NE], [-1, NE]], channel_multiplier=0
                                    ).then_inc(earlier_ready, 1)
            nc.gpsimd.memset(state[:, :, :, :], 0.0).then_inc(state_zero, 1)
            nc.gpsimd.memset(xm[:, :, :, :], 0.0).then_inc(halo_zero, 1)
            pool.wait_ge(state_zero, 1)
            pool.wait_ge(halo_zero, 1)

            def front(s, m):
                b = m[1]
                if s == 13:
                    pool.wait_ge(sp_masked, count(1, m, 1))
                    nc.gpsimd.tensor_tensor(acc[:, :, :], sp_e[:, :, :], acc[:, :, :], ALU.subtract).then_inc(sp_rest, 1)
                    pool.wait_ge(sp_rest, count(1, m, 1))
                    nc.gpsimd.tensor_tensor(sp_l[:, :, :], sp_l[:, :, :], acc[:, :, :], ALU.add).then_inc(sp_log, 1)

            def main(s, n):
                b, r, g = n[1], s % RB, s // G
                pool.wait_ge(scan_done, count(S, n, s + 1))
                if s % G == 0:
                    pool.wait_ge(c_loaded[g % RINGG], count(16 * NG // RINGG, n, 16 * (g // RINGG + 1)))
                pool.wait_ge(y_summed, count(S, n, s + 1 - RB))
                nc.gpsimd.tensor_tensor(hC[:, r], h[:, r],
                                        bC[:, g % RINGG, s % G:s % G + 1, :].to_broadcast([P, NJ, T]),
                                        ALU.mult).then_inc(hc_done, 1)
                nc.gpsimd.tensor_copy(state[:, b, :, s:s + 1], h[:, r, :, T - 1:T]).then_inc(state_saved, 1)

            def back(s, m):
                if s == 2:
                    pool.wait_ge(xb_loaded, count(16, m, 16))
                    pool.wait_ge(x1_done, count(1, m, 1))
                    pool.wait_ge(x2_done, count(1, m, 0))
                    nc.gpsimd.tensor_tensor(x1x[:, :, :], x1[:, :, :], xb[:, :, :], ALU.add).then_inc(x1x_done, 1)

            drive(pool, front, main, back)

        @block.scalar
        def _(act):
            def load_xf(m):
                act.wait_ge(xn_done, count(1, m, 0))
                act.dma_start(xf[:, :, :], x_v[m[0], m[1]]).then_inc(xf_loaded, 16)

            load_xf((0, 0))
            act.wait_ge(loaded["par"], 16)
            act.wait_ge(consts_ready, 2)
            nc.scalar.activation(exp_a[:, :, :], par[:, C_ALOG:C_ALOG + NJ * S].rearrange("p (j s) -> p j s", s=S),
                                 ACT.Exp).then_inc(a_exp, 1)

            def inv_std(k, m):
                act.wait_ge(stats[k], count(1, m, 1))
                nc.scalar.activation(lnv[k][:, :], mv[k][:, :, 1], ACT.Ln, bias=eps_c[:, :]).then_inc(lnv_done[k], 1)
                act.wait_ge(lnv_done[k], count(1, m, 1))
                nc.scalar.activation(rstd[k][:, :], lnv[k][:, :], ACT.Exp, scale=-0.5).then_inc(rstd_done[k], 1)

            def front(s, m):
                b = m[1]
                if s == 0 and not is_first(m):
                    load_xf(m)
                if s == 1:
                    inv_std(0, m)
                if s == 2:
                    inv_std(1, m)
                if s == 3:
                    ps = front_bank("uT")
                    act.wait_ge(filled_f, front_use("uT", m))
                    nc.scalar.activation(uT[:, 0, :], ps[:, 0, :], ACT.Identity, scale=pcol(C_LN1W), bias=pcol(C_LN1B))
                    nc.scalar.activation(uT[:, 1, :], ps[:, 1, :], ACT.Identity, scale=pcol(C_LN1W + 1),
                                         bias=pcol(C_LN1B + 1)).then_inc(uT_done, 1)
                if s == 4:
                    if is_first(m):
                        act.wait_ge(halo_zero, 1)
                    act.wait_ge(conv_tap, count(NJ * TAPS, m, -NJ * TAPS))
                    nc.scalar.activation(xm[:, b, :, 0:TAPS - 1], xm[:, b, :, T:T + TAPS - 1], ACT.Copy
                                         ).then_inc(halo_moved, 1)
                if s == 5:
                    act.wait_ge(yg_done, count(1, m, -1))
                    for i in range(2):
                        ps = front_bank(f"z{i}")
                        act.wait_ge(filled_f, front_use(f"z{i}", m))
                        nc.scalar.activation(sz[:, b, 2 * i:2 * i + 2, :], ps[:, :, :], ACT.Silu
                                             ).then_inc(sz_done, 1)
                if s == 6:
                    act.wait_ge(halo_moved, count(1, m, 1))
                    for i in range(2):
                        ps = front_bank(f"x{i}")
                        act.wait_ge(filled_f, front_use(f"x{i}", m))
                        nc.scalar.activation(xm[:, b, 2 * i:2 * i + 2, TAPS - 1:], ps[:, :, :], ACT.Copy
                                             ).then_inc(xm_done, 1)
                if s == 8:
                    act.wait_ge(conv_tap, count(NJ * TAPS, m, NJ * TAPS))
                    act.wait_ge(y_skip, count(1, m, -1))
                    nc.scalar.activation(xc[:, b, :, :], acc[:, :, :], ACT.Silu).then_inc(xc_done, 1)
                if s == 9:
                    ps = front_bank("low")
                    act.wait_ge(filled_f, front_use("low", m))
                    act.wait_ge(bc_stored, count(16, m, 0))
                    nc.scalar.activation(bc[:, :], ps[0:2 * S, 1, :], ACT.Copy).then_inc(bc_done, 1)
                    nc.scalar.activation(low[:, :], ps[:, 0, :], ACT.Copy).then_inc(low_done, 1)
                if s == 10:
                    act.wait_ge(scan_done, count(S, m, -S))
                    act.wait_ge(bx_done, count(S, m, -S))
                    act.wait_ge(sp_rest, count(1, m, 0))
                    for i in range(2):
                        ps = front_bank(f"dt{i}")
                        act.wait_ge(filled_f, front_use(f"dt{i}", m))
                        for k in range(2):
                            j = 2 * i + k
                            nc.scalar.activation(sp_e[:, j, :], ps[:, k, :], ACT.Abs, bias=pcol(C_DTB + j))
                            last = nc.scalar.activation(dt[:, b, j, :], ps[:, k, :], ACT.Relu, bias=pcol(C_DTB + j))
                        last.then_inc(relu_done, 1)
                if s == 11:
                    act.wait_ge(relu_done, count(2, m, 2))
                    nc.scalar.activation(sp_e[:, :, :], sp_e[:, :, :], ACT.Exp, scale=-1.0).then_inc(sp_exp, 1)
                    act.wait_ge(sp_one, count(1, m, 1))
                    nc.scalar.activation(sp_l[:, :, :], sp_l[:, :, :], ACT.Ln).then_inc(sp_ln, 1)

            def main(s, n):
                b, r = n[1], s % RB
                if s == 0:
                    act.wait_ge(dt_done, count(1, n, 1))
                    if is_first(n):
                        act.wait_ge(a_ready, 1)
                act.wait_ge(scan_done, count(S, n, s + 1 - RB))
                for j in range(NJ):
                    last = nc.scalar.activation(dA[:, r, j, :], dt[:, b, j, :], ACT.Exp, scale=neg_a[:, j, s:s + 1])
                last.then_inc(exp_done, 1)

            def back(s, m):
                if s == 0:
                    act.wait_ge(x1x_done, count(1, m, 0))
                    act.dma_start(xb[:, :, :], x_v[m[0], m[1]]).then_inc(xb_loaded, 16)
                if s == 2:
                    inv_std(2, m)
                if s == 3:
                    ps = back_bank("vT")
                    act.wait_ge(filled_b, back_use("vT", m))
                    nc.scalar.activation(vT[:, 0, :], ps[:, 0, :], ACT.Identity, scale=pcol(C_LN2W), bias=pcol(C_LN2B))
                    nc.scalar.activation(vT[:, 1, :], ps[:, 1, :], ACT.Identity, scale=pcol(C_LN2W + 1),
                                         bias=pcol(C_LN2B + 1)).then_inc(vT_done, 1)
                if s in (4, 5):
                    for i in (2 * (s - 4), 2 * (s - 4) + 1):
                        ps = back_bank(f"ff{i}")
                        act.wait_ge(filled_b, back_use(f"ff{i}", m))
                        act.wait_ge(hg_done, count(F1, m, i - 1))
                        nc.scalar.activation(gate[:, i % 2, :], ps[:, 1, :], ACT.Silu).then_inc(gate_done, 1)
                if s == 7:
                    inv_std(3, m)
                if s == 8:
                    act.wait_ge(nrm_done, count(1, m, 1))
                    nc.scalar.activation(lnn[:, :], nrm[:, 2, :], ACT.Ln, scale=float(2 ** LIFT)).then_inc(lnn_done, 1)
                    act.wait_ge(lnn_done, count(1, m, 1))
                    nc.scalar.activation(rn[:, :], lnn[:, :], ACT.Exp, scale=-0.5, bias=lift_c[:, :]).then_inc(rn_done, 1)
                    ps = back_bank("xeT")
                    act.wait_ge(filled_b, back_use("xeT", m))
                    nc.scalar.activation(xeT[:, :, :], ps[:, :, :], ACT.Copy).then_inc(xeT_done, 1)
                if s == 9:
                    act.wait_ge(lgm_done, count(1, m, 1))
                    nc.scalar.activation(pr[:, :, :], lgm[:, :, :], ACT.Exp).then_inc(pr_done, 1)
                if s == 10:
                    ps = back_bank("cT")
                    act.wait_ge(filled_b, back_use("cT", m))
                    act.wait_ge(cw_stored, count(16, m, 0))
                    nc.scalar.activation(cT[:, :], ps[0:NE].rearrange("p k t -> p (k t)")[:, 0:T], ACT.Copy
                                         ).then_inc(cT_done, 1)

            drive(act, front, main, back)

        @block.vector
        def _(dve):
            nc.vector.memset(eps_c[:, :], EPS).then_inc(consts_ready, 1)
            nc.vector.memset(lift_c[:, :], 0.5 * LIFT * math.log(2.0)).then_inc(consts_ready, 1)
            dve.wait_ge(loaded["par"], 16)
            dve.wait_ge(a_exp, 1)
            nc.vector.tensor_scalar(neg_a[:, :, :], exp_a[:, :, :], -1.0, None, ALU.mult).then_inc(a_ready, 1)
            dve.wait_ge(state_zero, 1)

            links = {"f": 0, "b": 0}

            def link(which, m, ins):
                chain, per = (front_chain, LINKS_FRONT) if which == "f" else (back_chain, LINKS_BACK)
                links[which] = links[which] % per + 1
                ins.then_inc(chain, 1)
                dve.wait_ge(chain, count(per, m, links[which]))

            def norm_stats(k, src, which, m):
                for j in range(SUB):
                    last = nc.vector.bn_stats(bn[k][:, j, :], src[:, j, :])
                link(which, m, last)
                nc.vector.memset(pause[:, :], 0.0)
                for j in range(SUB):
                    last = nc.vector.bn_aggr(mv[k][:, j, :], bn[k][:, j, :])
                last.then_inc(stats[k], 1)

            def normalise(k, dst, src, done, m):
                dve.wait_ge(rstd_done[k], count(1, m, 1))
                for j in range(SUB):
                    last = nc.vector.tensor_scalar(dst[:, j, :], src[:, j, :], mv[k][:, j, 0:1], rstd[k][:, j:j + 1],
                                                   ALU.subtract, ALU.mult)
                last.then_inc(done, 1)

            def front(s, m):
                b = m[1]
                if s == 1:
                    dve.wait_ge(xf_loaded, count(16, m, 16))
                    norm_stats(0, xf, "f", m)
                if s == 2:
                    dve.wait_ge(x1_done, count(1, m, -1))
                    normalise(0, xn[:, b], xf, xn_done, m)
                    dve.wait_ge(xn_done, count(1, m, 1))
                    norm_stats(1, xn[:, b], "f", m)
                if s == 3:
                    dve.wait_ge(filled_f, front_use_before("uT", m))
                    normalise(1, un, xn[:, b], un_done, m)
                if s == 7:
                    dve.wait_ge(xm_done, count(2, m, 2))
                    dve.wait_ge(sp_log, count(1, m, 0))
                    for tap in range(TAPS):
                        k = TAPS - 1 - tap
                        for j in range(NJ):
                            done = tap * NJ + j
                            w = pcol(C_CONVW + j * TAPS + k)
                            if tap == 0:
                                ins = nc.vector.tensor_scalar(acc[:, j, :], xm[:, b, j, k:k + T], w,
                                                              pcol(C_CONVB + j), ALU.mult, ALU.add)
                            else:
                                dve.wait_ge(conv_tap, count(NJ * TAPS, m, done - NJ + 1))
                                ins = nc.vector.scalar_tensor_tensor(out=acc[:, j, :], in0=xm[:, b, j, k:k + T],
                                                                     scalar=w, in1=acc[:, j, :],
                                                                     op0=ALU.mult, op1=ALU.add)
                            ins.then_inc(conv_tap, 1)
                if s == 11:
                    dve.wait_ge(sp_exp, count(1, m, 1))
                    nc.vector.tensor_scalar(sp_l[:, :, :], sp_e[:, :, :], 1.0, None, ALU.add).then_inc(sp_one, 1)
                    dve.wait_ge(xc_done, count(1, m, 1))
                    nc.vector.tensor_scalar(acc[:, :, :], sp_e[:, :, :], 1.0, -1.0, ALU.add, ALU.add
                                            ).then_inc(sp_back, 1)
                if s == 12:
                    dve.wait_ge(sp_ln, count(1, m, 1))
                    dve.wait_ge(sp_back, count(1, m, 1))
                    nc.vector.scalar_tensor_tensor(out=sp_l[:, :, :], in0=acc[:, :, :], scalar=0.0, in1=sp_l[:, :, :],
                                                   op0=ALU.is_gt, op1=ALU.mult).then_inc(sp_masked, 1)
                if s == 14:
                    dve.wait_ge(sp_log, count(1, m, 1))
                    nc.vector.tensor_tensor(dt[:, b], dt[:, b], sp_l[:, :, :], ALU.add).then_inc(dt_done, 1)
                    dve.wait_ge(dt_done, count(1, m, 1))
                    link("f", m, nc.vector.tensor_tensor(u[:, b], dt[:, b], xc[:, b], ALU.mult))

            def product(s, n):
                b, r, g = n[1], s % RB, s // G
                if s % G == 0:
                    dve.wait_ge(b_loaded[g % RINGG], count(16 * NG // RINGG, n, 16 * (g // RINGG + 1)))
                dve.wait_ge(scan_done, count(S, n, s + 1 - RB))
                nc.vector.tensor_tensor(bx[:, r], u[:, b],
                                        bB[:, g % RINGG, s % G:s % G + 1, :].to_broadcast([P, NJ, T]),
                                        ALU.mult).then_inc(bx_done, 1)

            def main(s, n):
                b, r = n[1], s % RB
                if s == 0:
                    product(0, n)
                if s < S - 1:
                    product(s + 1, n)
                dve.wait_ge(bx_done, count(S, n, s + 1))
                dve.wait_ge(exp_done, count(S, n, s + 1))
                dve.wait_ge(hc_done, count(S, n, s + 1 - RB))
                dve.wait_ge(state_saved, count(S, n, s + 1 - RB))
                for j in range(NJ):
                    last = nc.vector.tensor_tensor_scan(h[:, r, j, :], dA[:, r, j, :], bx[:, r, j, :],
                                                        state[:, b, j, s:s + 1], ALU.mult, ALU.add)
                last.then_inc(scan_done, 1)

            def back(s, m):
                b = m[1]
                if s == 0:
                    dve.wait_ge(y_summed, count(S, m, S))
                    dve.wait_ge(filled_b, back_use_before("op", m))
                    for j in range(NJ):
                        last = nc.vector.scalar_tensor_tensor(out=yg[:, j, :], in0=xc[:, b, j, :],
                                                              scalar=pcol(C_DSKIP + j), in1=psy[j // 2][:, j % 2, :],
                                                              op0=ALU.mult, op1=ALU.add)
                    last.then_inc(y_skip, 1)
                    dve.wait_ge(y_skip, count(1, m, 1))
                    nc.vector.tensor_tensor(yg[:, :, :], yg[:, :, :], sz[:, b], ALU.mult).then_inc(yg_done, 1)
                if s == 2:
                    ps = back_bank("op")
                    dve.wait_ge(filled_b, back_use("op", m))
                    dve.wait_ge(x1x_done, count(1, m, 0))
                    nc.vector.tensor_tensor(x1[:, :, :], xn[:, b], ps[:, :, :], ALU.add).then_inc(x1_done, 1)
                    dve.wait_ge(x1_done, count(1, m, 1))
                    norm_stats(2, x1, "b", m)
                if s == 3:
                    dve.wait_ge(filled_b, back_use_before("vT", m))
                    normalise(2, vn, x1, vn_done, m)
                if s in (4, 5):
                    for i in (2 * (s - 4), 2 * (s - 4) + 1):
                        ps = back_bank(f"ff{i}")
                        dve.wait_ge(filled_b, back_use(f"ff{i}", m))
                        dve.wait_ge(gate_done, count(F1, m, i + 1))
                        if i == 0:
                            dve.wait_ge(filled_b, back_use_before("fo", m))
                        nc.vector.tensor_tensor(hg[:, i, :], gate[:, i % 2, :], ps[:, 0, :], ALU.mult
                                                ).then_inc(hg_done, 1)
                if s == 7:
                    ps = back_bank("fo")
                    dve.wait_ge(filled_b, back_use("fo", m))
                    dve.wait_ge(x1x_done, count(1, m, 1))
                    dve.wait_ge(fin_done, count(1, m, 0))
                    nc.vector.tensor_tensor(x2[:, :, :], x1x[:, :, :], ps[:, :, :], ALU.add).then_inc(x2_done, 1)
                    dve.wait_ge(x2_done, count(1, m, 1))
                    norm_stats(3, x2, "b", m)
                if s == 8:
                    dve.wait_ge(filled_b, back_use_before("xeT", m))
                    normalise(3, xe, x2, xe_done, m)
                    var = mv[3][:, :, 1]
                    link("b", m, nc.vector.scalar_tensor_tensor(out=nrm[:, 0, :], in0=var, scalar=float(DM),
                                                                in1=rstd[3][:, :], op0=ALU.mult, op1=ALU.mult))
                    link("b", m, nc.vector.tensor_tensor(nrm[:, 1, :], nrm[:, 0, :], rstd[3][:, :], ALU.mult))
                    nc.vector.tensor_scalar(nrm[:, 2, :], nrm[:, 1, :], NORM_FLOOR * NORM_FLOOR, None, ALU.max
                                            ).then_inc(nrm_done, 1)
                if s == 9:
                    ps = back_bank("rt")
                    dve.wait_ge(filled_b, back_use("rt", m))
                    dve.wait_ge(rn_done, count(1, m, 1))
                    for j in range(SUB):
                        last = nc.vector.tensor_scalar(lg[:, j, :], ps[:, 0, j * NE:(j + 1) * NE], rn[:, j:j + 1], None,
                                                       ALU.mult)
                    link("b", m, last)
                    link("b", m, nc.vector.reduce_max(mx[:, :], lg[:, :, :], X))
                    nc.vector.tensor_tensor(lgm[:, :, :], lg[:, :, :], mx[:, :].unsqueeze(2).to_broadcast([P, SUB, NE]),
                                            ALU.subtract).then_inc(lgm_done, 1)
                    dve.wait_ge(pr_done, count(1, m, 1))
                    p_j = pr[:, :, :].unsqueeze(2).to_broadcast([P, SUB, NE, NE])
                    p_e = pr[:, :, :].unsqueeze(3).to_broadcast([P, SUB, NE, NE])
                    nc.vector.tensor_tensor(gt[:, :, :, :], p_j, p_e, ALU.is_gt)
                    link("b", m, nc.vector.tensor_tensor(eq[:, :, :, :], p_j, p_e, ALU.is_equal))
                    if is_first(m):
                        dve.wait_ge(earlier_ready, 1)
                    link("b", m, nc.vector.tensor_tensor(eq[:, :, :, :], eq[:, :, :, :],
                                                         earlier[:, :, :].unsqueeze(1).to_broadcast([P, SUB, NE, NE]),
                                                         ALU.mult))
                    link("b", m, nc.vector.tensor_tensor(gt[:, :, :, :], gt[:, :, :, :], eq[:, :, :, :], ALU.add))
                    link("b", m, nc.vector.reduce_sum(rank[:, :, :], gt[:, :, :, :], X))
                    link("b", m, nc.vector.scalar_tensor_tensor(out=psel[:, :, :], in0=rank[:, :, :], scalar=1.5,
                                                                in1=pr[:, :, :], op0=ALU.is_lt, op1=ALU.mult))
                    link("b", m, nc.vector.reduce_sum(den[:, :], psel[:, :, :], X))
                    link("b", m, nc.vector.reciprocal(rden[:, :], den[:, :]))
                    dve.wait_ge(filled_b, back_use_before("cT", m))
                    nc.vector.tensor_tensor(cw[:, :, :], psel[:, :, :], rden[:, :].unsqueeze(2).to_broadcast([P, SUB, NE]),
                                            ALU.mult).then_inc(cw_done, 1)
                if s in (12, 13):
                    for i in (2 * (s - 12), 2 * (s - 12) + 1):
                        ps = back_bank(f"wa{i}")
                        dve.wait_ge(filled_b, back_use(f"wa{i}", m))
                        if i == 0:
                            dve.wait_ge(cbc_loaded, count(16, m, 16))
                            dve.wait_ge(filled_b, back_use_before("wb", m))
                        nc.vector.tensor_tensor(hE[:, 2 * i:2 * i + 2, :], cbc[:, 2 * i:2 * i + 2, :], ps[:, :, :],
                                                ALU.mult).then_inc(hE_done, 1)
                if s == 15:
                    ps = back_bank("wb")
                    dve.wait_ge(filled_b, back_use("wb", m))
                    dve.wait_ge(out_stored, count(16, m, 0))
                    nc.vector.tensor_tensor(fin[:, :, :], x2[:, :, :], ps[:, :, :], ALU.add).then_inc(fin_done, 1)

            drive(dve, front, main, back)

        @block.tensor
        def _(pe):
            mm = nc.tensor.matmul
            pe.wait_ge(ident_ready, 1)

            def transposes(dst, src):
                for k in range(KM):
                    for j in range(SUB):
                        last = nc.tensor.transpose(dst[:, k, j * P:(j + 1) * P], src[:, j, k * P:(k + 1) * P], ident[:, :])
                return last

            def project(dst, w, rhs, kt, cols):
                for i, c in enumerate(cols):
                    for k in range(kt):
                        last = mm(dst[:, i, :], w[:, k, c:c + P], rhs[:, k, :], start=k == 0, stop=k == kt - 1)
                return last

            def project_tokens(dst, lhs, w, kt):
                for j in range(SUB):
                    for k in range(kt):
                        last = mm(dst[:, j, :], lhs[:, k, j * P:(j + 1) * P], w[:, k, :], start=k == 0, stop=k == kt - 1)
                return last

            def first(m, key):
                if is_first(m):
                    pe.wait_ge(loaded[key], 16)

            def front(s, m):
                b = m[1]
                if s == 3:
                    ps = front_bank("uT")
                    pe.wait_ge(relu_done, count(2, m, -1))
                    pe.wait_ge(un_done, count(1, m, 1))
                    transposes(ps, un).then_inc(filled_f, 1)
                if s == 5:
                    first(m, "in")
                    pe.wait_ge(uT_done, count(1, m, 1))
                    for i in range(2):
                        ps = front_bank(f"z{i}")
                        pe.wait_ge(low_done if i else relu_done, count(1, m, 0) if i else count(2, m, 0))
                        project(ps, w_in_sb, uT, KM, [DI + (2 * i + k) * P for k in range(2)]
                                ).then_inc(filled_f, 1)
                if s == 6:
                    for i in range(2):
                        ps = front_bank(f"x{i}")
                        pe.wait_ge(sz_done if i else uT_done, count(2, m, 1) if i else count(1, m, 1))
                        project(ps, w_in_sb, uT, KM, [(2 * i + k) * P for k in range(2)]
                                ).then_inc(filled_f, 1)
                if s == 9:
                    first(m, "x")
                    pe.wait_ge(xc_done, count(1, m, 1))
                    ps = front_bank("low")
                    pe.wait_ge(sz_done, count(2, m, 2))
                    for k in range(NJ):
                        mm(ps[0:2 * S, 1, :], w_x_sb[:, k, DTR:DTR + 2 * S], xc[:, b, k, :], start=k == 0, stop=k == NJ - 1)
                    for k in range(NJ):
                        last = mm(ps[:, 0, :], w_x_sb[:, k, 0:DTR], xc[:, b, k, :], start=k == 0, stop=k == NJ - 1)
                    last.then_inc(filled_f, 1)
                if s == 10:
                    first(m, "dt")
                    pe.wait_ge(low_done, count(1, m, 1))
                    for i in range(2):
                        ps = front_bank(f"dt{i}")
                        pe.wait_ge(xm_done, count(2, m, i + 1))
                        for k in range(2):
                            j = 2 * i + k
                            last = mm(ps[:, k, :], w_dt_sb[:, j * P:(j + 1) * P], low[:, :], start=True, stop=True)
                        last.then_inc(filled_f, 1)

            def sum_states(s, n):
                r = s % RB
                pe.wait_ge(hc_done, count(S, n, s + 1))
                if s == 0:
                    pe.wait_ge(y_skip, count(1, n, 0))
                for i in range(2):
                    last = mm(psy[i][:, :, :], ident[:, :], hC[:, r, 2 * i:2 * i + 2, :], start=s == 0, stop=s == S - 1)
                last.then_inc(y_summed, 1)

            def main(s, n):
                if s > 0:
                    sum_states(s - 1, n)

            def back(s, m):
                if s == 0:
                    sum_states(S - 1, m)
                if s == 1:
                    first(m, "out")
                    ps = back_bank("op")
                    pe.wait_ge(hE_done, count(NE // 2, m, -1))
                    pe.wait_ge(yg_done, count(1, m, 1))
                    project_tokens(ps, yg, w_out_sb, NJ).then_inc(filled_b, 1)
                if s == 3:
                    ps = back_bank("vT")
                    pe.wait_ge(hE_done, count(NE // 2, m, 0))
                    pe.wait_ge(vn_done, count(1, m, 1))
                    transposes(ps, vn).then_inc(filled_b, 1)
                if s in (4, 5):
                    first(m, "ff")
                    pe.wait_ge(vT_done, count(1, m, 1))
                    for i in (2 * (s - 4), 2 * (s - 4) + 1):
                        ps = back_bank(f"ff{i}")
                        pe.wait_ge((fin_done, x1_done, vT_done, hg_done)[i], count(1, m, min(i, 1)) if i < 3 else count(F1, m, 1))
                        project(ps, w_ff_sb, vT, KM, [i * P, HID // 2 + i * P]).then_inc(filled_b, 1)
                if s == 6:
                    first(m, "fo")
                    ps = back_bank("fo")
                    pe.wait_ge(hg_done, count(F1, m, 2))
                    pe.wait_ge(hg_done, count(F1, m, F1))
                    project_tokens(ps, hg, w_fo_sb, F1).then_inc(filled_b, 1)
                if s == 8:
                    ps = back_bank("xeT")
                    pe.wait_ge(hg_done, count(F1, m, 3))
                    pe.wait_ge(xe_done, count(1, m, 1))
                    transposes(ps, xe).then_inc(filled_b, 1)
                if s == 9:
                    first(m, "r")
                    pe.wait_ge(xeT_done, count(1, m, 1))
                    ps = back_bank("rt")
                    pe.wait_ge(hg_done, count(F1, m, 4))
                    for j in range(SUB):
                        for k in range(KM):
                            last = mm(ps[:, 0, j * NE:(j + 1) * NE], xeT[:, k, j * P:(j + 1) * P], w_r_sb[:, k, :],
                                      start=k == 0, stop=k == KM - 1)
                    last.then_inc(filled_b, 1)
                if s == 10:
                    ps = back_bank("cT")
                    pe.wait_ge(x2_done, count(1, m, 1))
                    pe.wait_ge(cw_done, count(1, m, 1))
                    for j in range(SUB):
                        last = nc.tensor.transpose(ps[0:NE, 0, j * P:(j + 1) * P], cw[:, j, :], ident[:, :])
                    last.then_inc(filled_b, 1)
                if s in (12, 13):
                    first(m, "a")
                    for i in (2 * (s - 12), 2 * (s - 12) + 1):
                        ps = back_bank(f"wa{i}")
                        pe.wait_ge((xeT_done, lgm_done, cT_done, hE_done)[i], count(1, m, 1) if i < 3 else count(NE // 2, m, 1))
                        project(ps, w_a_sb, xeT, KM, [2 * i * RANK, (2 * i + 1) * RANK]
                                ).then_inc(filled_b, 1)
                if s == 14:
                    first(m, "b")
                    ps = back_bank("wb")
                    pe.wait_ge(hE_done, count(NE // 2, m, 2))
                    pe.wait_ge(hE_done, count(NE // 2, m, NE // 2))
                    project_tokens(ps, hE, w_b_sb, NE).then_inc(filled_b, 1)

            drive(pe, front, main, back)


def kernel(**inputs):
    import numpy as np
    import concourse.bacc as bacc
    from concourse.bass_utils import run_bass_kernel_spmd

    def get(name):
        return np.asarray(inputs[name])

    def tiles(w):
        k, m = w.shape
        return np.ascontiguousarray(w.reshape(k // P, P, m).transpose(1, 0, 2).reshape(P, -1))

    def columns(v):
        return tiles(v.reshape(v.shape[0], -1))

    params = np.ascontiguousarray(np.concatenate([
        columns(get("L0_attn_conv_w")), columns(get("L0_attn_conv_b")), columns(get("L0_attn_dt_proj_b")),
        columns(get("L0_attn_D_skip")), columns(get("L0_attn_A_log")),
        columns(get("L0_attn_ln1_w")), columns(get("L0_attn_ln1_b")),
        columns(get("L0_attn_ln2_w")), columns(get("L0_attn_ln2_b"))], axis=1))
    arrays = {
        "x": np.ascontiguousarray(get("L0_attn_x")),
        "params": params,
        "w_in": tiles(get("L0_attn_in_proj_w").T),
        "w_x": tiles(get("L0_attn_x_proj_w").T),
        "w_dt": tiles(get("L0_attn_dt_proj_w").T),
        "w_out": tiles(get("L0_attn_out_proj_w").T),
        "w_ff": tiles(get("L0_attn_ff_proj_w").T),
        "w_fo": tiles(get("L0_attn_ff_out_w").T),
        "w_a": tiles(get("L0_ffn_Wa").transpose(1, 0, 2).reshape(DM, NE * RANK)),
        "w_b": tiles(get("L0_ffn_Wb").reshape(NE * RANK, DM)),
        "w_r": tiles(get("L0_ffn_router_w")),
    }
    f32 = mybir.dt.float32
    nc = bacc.Bacc("TRN2", target_bir_lowering=False, num_devices=1)
    aps = {k: nc.dram_tensor(f"in_{k}", a.shape, f32, kind="ExternalInput").ap() for k, a in arrays.items()}
    bc_scratch = nc.dram_tensor("bc_scratch", (2 * S, T), f32, kind="Internal").ap()
    cw_scratch = nc.dram_tensor("cw_scratch", (NE, T), f32, kind="Internal").ap()
    out = nc.dram_tensor("out_0", (B, L, DM), f32, kind="ExternalOutput").ap()
    mamba_moe(nc, aps["x"], aps["params"], aps["w_in"], aps["w_x"], aps["w_dt"], aps["w_out"], aps["w_ff"],
              aps["w_fo"], aps["w_a"], aps["w_b"], aps["w_r"], bc_scratch, cw_scratch, out)
    r = run_bass_kernel_spmd(nc, [{f"in_{k}": a for k, a in arrays.items()}], core_ids=[0])
    return r.results[0]["out_0"]
```

```python
import math
from contextlib import ExitStack

import concourse.bass as bass
from concourse import mybir

B, L, DM, DI, S, TAPS, DTR, HID = 2, 2048, 256, 512, 16, 4, 128, 1024
NE, RANK = 8, 128
P = 128
T = 256
SUB = T // P
KM = DM // P
NJ = DI // P
NC = L // T
G = 4
NG = S // G
RINGG = 2
RB = 2
RA = 4
F1 = HID // 2 // P
EPS = 1e-5
NORM_FLOOR = 1e-12
LIFT = 20

C_CONVW, C_CONVB, C_DTB, C_DSKIP, C_ALOG = 0, NJ * TAPS, NJ * TAPS + NJ, NJ * TAPS + 2 * NJ, NJ * TAPS + 3 * NJ
C_LN1W = C_ALOG + NJ * S
C_LN1B, C_LN2W, C_LN2B = C_LN1W + KM, C_LN1W + 2 * KM, C_LN1W + 3 * KM
NPAR = C_LN1W + 4 * KM

FRONT_UNITS = ["uT", "x0", "x1", "z0", "z1", "low", "dt0", "dt1"]
BACK_UNITS = ["op", "vT", "G0", "G1", "A0", "A1", "fo", "xeT", "rt", "cT", "wa0", "wa1", "wa2", "wa3", "wb"]
RING = 3

LINKS_FRONT = 2 + 1
LINKS_BACK = 2 + 2 + 9


def count(per_step, step, k):
    c, b = step
    value = c * (2 * per_step) + (per_step * b + k)
    return max(value, 0) if isinstance(value, int) else value


def is_first(step):
    return isinstance(step[0], int) and step == (0, 0)


def is_last(step):
    return isinstance(step[0], int) and step == (NC - 1, B - 1)


def prev(step):
    c, b = step
    return (c, 0) if b else (c - 1, 1)


def drive(eng, front, main, back):
    def step(before, now, after):
        for s in range(S):
            if now:
                main(s, now)
            if before:
                back(s, before)
            if after:
                front(s, after)

    step(None, None, (0, 0))
    step(None, (0, 0), (0, 1))
    step((0, 0), (0, 1), (1, 0))
    with eng.Fori(1, NC - 1) as c:
        step((c - 1, 1), (c, 0), (c, 1))
        step((c, 0), (c, 1), (c + 1, 0))
    step((NC - 2, 1), (NC - 1, 0), (NC - 1, 1))
    step((NC - 1, 0), (NC - 1, 1), None)
    step((NC - 1, 1), None, None)


def mamba_moe(nc, x, params, w_in, w_x, w_dt, w_out, w_ff, w_fo, w_a, w_b, w_r, bc_scratch, cw_scratch, out):
    f32 = mybir.dt.float32
    ALU = mybir.AluOpType
    ACT = mybir.ActivationFunctionType
    X = mybir.AxisListType.X

    x_v = x.rearrange("b (c j p) d -> c b p j d", p=P, j=SUB)
    out_v = out.rearrange("b (c j p) d -> c b p j d", p=P, j=SUB)

    ctx = ExitStack()
    with ctx:
        def sb(name, shape):
            return ctx.enter_context(nc.sbuf_tensor(name, shape, f32))

        def sem(name):
            return ctx.enter_context(nc.semaphore(name))

        par = sb("par", [P, NPAR])
        w_in_sb = sb("w_in_sb", [P, KM, 2 * DI])
        w_x_sb = sb("w_x_sb", [P, NJ, DTR + 2 * S])
        w_dt_sb = sb("w_dt_sb", [P, DI])
        w_out_sb = sb("w_out_sb", [P, NJ, DM])
        w_ff_sb = sb("w_ff_sb", [P, KM, HID])
        w_fo_sb = sb("w_fo_sb", [P, F1, DM])
        w_a_sb = sb("w_a_sb", [P, KM, NE * RANK])
        w_b_sb = sb("w_b_sb", [P, NE, DM])
        w_r_sb = sb("w_r_sb", [P, KM, NE])
        ident = sb("ident", [P, P])
        earlier = sb("earlier", [P, NE, NE])
        neg_a = sb("neg_a", [P, NJ, S])
        exp_a = sb("exp_a", [P, NJ, S])
        eps_c = sb("eps_c", [P, 1])
        lift_c = sb("lift_c", [P, 1])

        xf = sb("xf", [P, SUB, DM])
        xn = sb("xn", [P, B, SUB, DM])
        un = sb("un", [P, SUB, DM])
        uT = sb("uT", [P, KM, T])
        xm = sb("xm", [P, B, NJ, TAPS - 1 + T])
        acc = sb("acc", [P, NJ, T])
        xc = sb("xc", [P, B, NJ, T])
        sz = sb("sz", [P, B, NJ, T])
        low = sb("low", [P, T])
        bc = sb("bc", [2 * S, T])
        sp_e = sb("sp_e", [P, NJ, T])
        sp_l = sb("sp_l", [P, NJ, T])
        dt = sb("dt", [P, B, NJ, T])
        u = sb("u", [P, B, NJ, T])
        bn = [sb(f"bn{k}", [P, SUB, 6]) for k in range(4)]
        mv = [sb(f"mv{k}", [P, SUB, 2]) for k in range(4)]
        lnv = [sb(f"lnv{k}", [P, SUB]) for k in range(4)]
        rstd = [sb(f"rstd{k}", [P, SUB]) for k in range(4)]

        pause = sb("pause", [P, 1])

        bB = sb("bB", [P, RINGG, G, T])
        bC = sb("bC", [P, RINGG, G, T])
        dA = sb("dA", [P, RA, NJ, T])
        bx = sb("bx", [P, RB, NJ, T])
        h = sb("h", [P, RB, NJ, T])
        hC = sb("hC", [P, RB, NJ, T])
        state = sb("state", [P, B, NJ, S])

        xb = sb("xb", [P, SUB, DM])
        yg = sb("yg", [P, NJ, T])
        x1 = sb("x1", [P, SUB, DM])
        x1x = sb("x1x", [P, SUB, DM])
        vn = sb("vn", [P, SUB, DM])
        vT = sb("vT", [P, KM, T])
        hg = sb("hg", [P, F1, T])
        x2 = sb("x2", [P, SUB, DM])
        xe = sb("xe", [P, SUB, DM])
        xeT = sb("xeT", [P, KM, T])
        nrm = sb("nrm", [P, 3, SUB])
        lnn = sb("lnn", [P, SUB])
        rn = sb("rn", [P, SUB])
        lg = sb("lg", [P, SUB, NE])
        lgm = sb("lgm", [P, SUB, NE])
        mx = sb("mx", [P, SUB])
        pr = sb("pr", [P, SUB, NE])
        gt = sb("gt", [P, SUB, NE, NE])
        eq = sb("eq", [P, SUB, NE, NE])
        rank = sb("rank", [P, SUB, NE])
        psel = sb("psel", [P, SUB, NE])
        den = sb("den", [P, SUB])
        rden = sb("rden", [P, SUB])
        cw = sb("cw", [P, SUB, NE])
        cT = sb("cT", [NE, T])
        cbc = sb("cbc", [P, NE, T])
        fin = sb("fin", [P, SUB, DM])

        psy = [ctx.enter_context(nc.psum_tensor(f"psy{i}", [P, 2, T], f32)) for i in range(2)]
        psf = [ctx.enter_context(nc.psum_tensor(f"psf{i}", [P, 2, T], f32)) for i in range(RING)]
        psb = [ctx.enter_context(nc.psum_tensor(f"psb{i}", [P, 2, T], f32)) for i in range(RING)]

        loaded = {k: sem(f"loaded_{k}") for k in ("par", "in", "x", "dt", "out", "ff", "fo", "a", "b", "r")}
        ident_zero, ident_ready = sem("ident_zero"), sem("ident_ready")
        earlier_one, earlier_ready = sem("earlier_one"), sem("earlier_ready")
        consts_ready, state_zero, halo_zero = sem("consts_ready"), sem("state_zero"), sem("halo_zero")
        a_exp, a_ready = sem("a_exp"), sem("a_ready")
        filled_f, filled_b = sem("filled_f"), sem("filled_b")
        xf_loaded, xb_loaded = sem("xf_loaded"), sem("xb_loaded")
        stats = [sem(f"stats{k}") for k in range(4)]
        lnv_done = [sem(f"lnv_done{k}") for k in range(4)]
        rstd_done = [sem(f"rstd_done{k}") for k in range(4)]
        xn_done, un_done, uT_done = sem("xn_done"), sem("un_done"), sem("uT_done")
        halo_moved, xm_done, conv_tap = sem("halo_moved"), sem("xm_done"), sem("conv_tap")
        sz_done, xc_done = sem("sz_done"), sem("xc_done")
        low_done, bc_done = sem("low_done"), sem("bc_done")
        bc_stored = sem("bc_stored")
        b_loaded = [sem(f"b_loaded{i}") for i in range(RINGG)]
        c_loaded = [sem(f"c_loaded{i}") for i in range(RINGG)]
        relu_done, sp_exp, sp_ln = sem("relu_done"), sem("sp_exp"), sem("sp_ln")
        sp_one, sp_masked = sem("sp_one"), sem("sp_masked")
        sp_back, sp_rest, sp_log = sem("sp_back"), sem("sp_rest"), sem("sp_log")
        dt_done, u_done = sem("dt_done"), sem("u_done")
        exp_done, bx_done, scan_done = sem("exp_done"), sem("bx_done"), sem("scan_done")
        hc_done, state_saved, y_summed = sem("hc_done"), sem("state_saved"), sem("y_summed")
        y_skip, yg_done = sem("y_skip"), sem("yg_done")
        x1_done, x1x_done = sem("x1_done"), sem("x1x_done")
        vn_done, vT_done = sem("vn_done"), sem("vT_done")
        gate_done, hg_done = sem("gate_done"), sem("hg_done")
        x2_done, xe_done, xeT_done = sem("x2_done"), sem("xe_done"), sem("xeT_done")
        nrm_done, lnn_done, rn_done = sem("nrm_done"), sem("lnn_done"), sem("rn_done")
        lgm_done, pr_done, cw_done, cT_done = sem("lgm_done"), sem("pr_done"), sem("cw_done"), sem("cT_done")
        cw_stored, cbc_loaded = sem("cw_stored"), sem("cbc_loaded")
        hE_done, fin_done, out_stored = sem("hE_done"), sem("fin_done"), sem("out_stored")
        front_chain, back_chain = sem("front_chain"), sem("back_chain")

        def pcol(col):
            return par[:, col:col + 1]

        def front_bank(name):
            return psf[FRONT_UNITS.index(name) % RING]

        def back_bank(name):
            return psb[BACK_UNITS.index(name) % RING]

        def front_use(name, m):
            return count(len(FRONT_UNITS), m, FRONT_UNITS.index(name) + 1)

        def back_use(name, m):
            return count(len(BACK_UNITS), m, BACK_UNITS.index(name) + 1)

        def front_use_before(name, m):
            return count(len(FRONT_UNITS), m, FRONT_UNITS.index(name) + 1 - len(FRONT_UNITS))

        def back_use_before(name, m):
            return count(len(BACK_UNITS), m, BACK_UNITS.index(name) + 1 - len(BACK_UNITS))

        block = ctx.enter_context(nc.Block())

        @block.sync
        def _(sp):
            def flat(w):
                return w[:, :, :].rearrange("p k m -> p (k m)") if len(w.shape) == 3 else w[:, :]

            sp.dma_start(par[:, :], params).then_inc(loaded["par"], 16)

            for key, dst, src in (("in", w_in_sb, w_in), ("x", w_x_sb, w_x), ("dt", w_dt_sb, w_dt)):
                sp.dma_start(flat(dst), src).then_inc(loaded[key], 16)
            late = [("out", w_out_sb, w_out), ("ff", w_ff_sb, w_ff), ("fo", w_fo_sb, w_fo), ("r", w_r_sb, w_r),
                    ("a", w_a_sb, w_a), ("b", w_b_sb, w_b)]

            def store_out(m):
                sp.wait_ge(fin_done, count(1, m, 1))
                sp.dma_start(out_v[m[0], m[1]], fin[:, :, :]).then_inc(out_stored, 16)

            def value(v):
                if not isinstance(v, int):
                    sp.compute_val(v)
                return v

            def load_group(m, g, read=None):
                if read is None:
                    read = value(count(S, m, G * (g - RINGG + 1)))
                sp.wait_ge(bx_done, read)
                sp.dma_start(bB[:, g % RINGG], bc_scratch[g * G:(g + 1) * G, :].partition_broadcast(P)
                             ).then_inc(b_loaded[g % RINGG], 16)
                sp.wait_ge(hc_done, read)
                sp.dma_start(bC[:, g % RINGG], bc_scratch[S + g * G:S + (g + 1) * G, :].partition_broadcast(P)
                             ).then_inc(c_loaded[g % RINGG], 16)

            def front(s, m):
                if s == 10:
                    spread, read = value(count(16 * NG // RINGG, m, 0)), value(count(1, m, 1))
                    for i in range(RINGG):
                        sp.wait_ge(b_loaded[i], spread)
                        sp.wait_ge(c_loaded[i], spread)
                    sp.wait_ge(bc_done, read)
                    sp.dma_start(bc_scratch, bc[:, :]).then_inc(bc_stored, 16)
                if s == 11:
                    stored, read = value(count(16, m, 16)), value(count(S, m, -G))
                    sp.wait_ge(bc_stored, stored)
                    load_group(m, 0, read)
                if s == 15 and is_first(m):
                    for key, dst, src in late:
                        sp.dma_start(flat(dst), src).then_inc(loaded[key], 16)

            def main(s, n):
                if s in (0, 4, 8):
                    load_group(n, 1 + s // 4)

            def back(s, m):
                if s == 0 and not is_first(m):
                    store_out(prev(m))
                if s == 12:
                    before, ready = value(count(16, m, 0)), value(count(1, m, 1))
                    stored, used = value(count(16, m, 16)), value(back_use_before("wb", m))
                    sp.wait_ge(cbc_loaded, before)
                    sp.wait_ge(cT_done, ready)
                    sp.dma_start(cw_scratch, cT[:, :]).then_inc(cw_stored, 16)
                    sp.wait_ge(cw_stored, stored)
                    sp.wait_ge(filled_b, used)
                    sp.dma_start(cbc[:, :, :], cw_scratch.partition_broadcast(P)).then_inc(cbc_loaded, 16)

            drive(sp, front, main, back)
            store_out((NC - 1, B - 1))
            sp.wait_ge(out_stored, 16 * B * NC)

        @block.gpsimd
        def _(pool):
            nc.gpsimd.memset(ident[:, :], 0.0).then_inc(ident_zero, 1)
            pool.wait_ge(ident_zero, 1)
            nc.gpsimd.affine_select(out=ident[:, :], in_=ident[:, :], compare_op=ALU.not_equal, fill=1.0,
                                    base=0, pattern=[[-1, P]], channel_multiplier=1).then_inc(ident_ready, 1)
            nc.gpsimd.memset(earlier[:, :, :], 1.0).then_inc(earlier_one, 1)
            pool.wait_ge(earlier_one, 1)
            nc.gpsimd.affine_select(out=earlier[:, :, :], in_=earlier[:, :, :], compare_op=ALU.is_gt, fill=0.0,
                                    base=0, pattern=[[1, NE], [-1, NE]], channel_multiplier=0
                                    ).then_inc(earlier_ready, 1)
            nc.gpsimd.memset(state[:, :, :, :], 0.0).then_inc(state_zero, 1)
            nc.gpsimd.memset(xm[:, :, :, :], 0.0).then_inc(halo_zero, 1)
            pool.wait_ge(state_zero, 1)
            pool.wait_ge(halo_zero, 1)

            def front(s, m):
                b = m[1]
                if s == 13:
                    pool.wait_ge(sp_masked, count(1, m, 1))
                    nc.gpsimd.tensor_tensor(acc[:, :, :], sp_e[:, :, :], acc[:, :, :], ALU.subtract).then_inc(sp_rest, 1)
                    pool.wait_ge(sp_rest, count(1, m, 1))
                    nc.gpsimd.tensor_tensor(sp_l[:, :, :], sp_l[:, :, :], acc[:, :, :], ALU.add).then_inc(sp_log, 1)

            def main(s, n):
                b, r, g = n[1], s % RB, s // G
                pool.wait_ge(scan_done, count(S, n, s + 1))
                if s % G == 0:
                    pool.wait_ge(c_loaded[g % RINGG], count(16 * NG // RINGG, n, 16 * (g // RINGG + 1)))
                pool.wait_ge(y_summed, count(S, n, s + 1 - RB))
                nc.gpsimd.tensor_tensor(hC[:, r], h[:, r],
                                        bC[:, g % RINGG, s % G:s % G + 1, :].to_broadcast([P, NJ, T]),
                                        ALU.mult).then_inc(hc_done, 1)
                nc.gpsimd.tensor_copy(state[:, b, :, s:s + 1], h[:, r, :, T - 1:T]).then_inc(state_saved, 1)

            def back(s, m):
                if s == 0:
                    pool.wait_ge(y_skip, count(1, m, 1))
                    nc.gpsimd.tensor_tensor(yg[:, :, :], yg[:, :, :], sz[:, m[1]], ALU.mult).then_inc(yg_done, 1)
                if s == 2:
                    pool.wait_ge(xb_loaded, count(16, m, 16))
                    pool.wait_ge(x1_done, count(1, m, 1))
                    pool.wait_ge(x2_done, count(1, m, 0))
                    nc.gpsimd.tensor_tensor(x1x[:, :, :], x1[:, :, :], xb[:, :, :], ALU.add).then_inc(x1x_done, 1)

            drive(pool, front, main, back)

        @block.scalar
        def _(act):
            def load_xf(m):
                act.wait_ge(xn_done, count(1, m, 0))
                act.dma_start(xf[:, :, :], x_v[m[0], m[1]]).then_inc(xf_loaded, 16)

            load_xf((0, 0))
            act.wait_ge(loaded["par"], 16)
            act.wait_ge(consts_ready, 2)
            nc.scalar.preload_act_table_set("natural_log_exp_and_others")
            nc.scalar.activation(exp_a[:, :, :], par[:, C_ALOG:C_ALOG + NJ * S].rearrange("p (j s) -> p j s", s=S),
                                 ACT.Exp).then_inc(a_exp, 1)

            def inv_std(k, m):
                act.wait_ge(stats[k], count(1, m, 1))
                nc.scalar.activation(lnv[k][:, :], mv[k][:, :, 1], ACT.Ln, bias=eps_c[:, :]).then_inc(lnv_done[k], 1)
                act.wait_ge(lnv_done[k], count(1, m, 1))
                nc.scalar.activation(rstd[k][:, :], lnv[k][:, :], ACT.Exp, scale=-0.5).then_inc(rstd_done[k], 1)

            def use_log_exp():
                nc.scalar.preload_act_table_set("natural_log_exp_and_others")

            def front(s, m):
                b = m[1]
                if s == 0 and not is_first(m):
                    load_xf(m)
                if s == 1:
                    inv_std(0, m)
                if s == 2:
                    inv_std(1, m)
                if s == 3:
                    if is_first(m):
                        act.wait_ge(halo_zero, 1)
                    act.wait_ge(conv_tap, count(NJ * TAPS, m, -NJ * TAPS))
                    nc.scalar.activation(xm[:, b, :, 0:TAPS - 1], xm[:, b, :, T:T + TAPS - 1], ACT.Copy
                                         ).then_inc(halo_moved, 1)
                    ps = front_bank("uT")
                    act.wait_ge(filled_f, front_use("uT", m))
                    nc.scalar.activation(uT[:, 0, :], ps[:, 0, :], ACT.Identity, scale=pcol(C_LN1W), bias=pcol(C_LN1B))
                    nc.scalar.activation(uT[:, 1, :], ps[:, 1, :], ACT.Identity, scale=pcol(C_LN1W + 1),
                                         bias=pcol(C_LN1B + 1)).then_inc(uT_done, 1)
                if s == 4:
                    act.wait_ge(halo_moved, count(1, m, 1))
                    for i in range(2):
                        ps = front_bank(f"x{i}")
                        act.wait_ge(filled_f, front_use(f"x{i}", m))
                        nc.scalar.activation(xm[:, b, 2 * i:2 * i + 2, TAPS - 1:], ps[:, :, :], ACT.Copy
                                             ).then_inc(xm_done, 1)
                if s == 7:
                    act.wait_ge(yg_done, count(1, m, -1))
                    act.wait_ge(y_skip, count(1, m, -1))
                    for i in range(2):
                        ps = front_bank(f"z{i}")
                        act.wait_ge(filled_f, front_use(f"z{i}", m))
                        nc.scalar.activation(sz[:, b, 2 * i:2 * i + 2, :], ps[:, :, :], ACT.Silu
                                             ).then_inc(sz_done, 1)
                    act.wait_ge(conv_tap, count(NJ * TAPS, m, NJ * TAPS))
                    nc.scalar.activation(xc[:, b, :, :], acc[:, :, :], ACT.Silu).then_inc(xc_done, 1)
                if s == 8 and is_first(m):
                    use_log_exp()
                if s == 9:
                    ps = front_bank("low")
                    act.wait_ge(filled_f, front_use("low", m))
                    act.wait_ge(bc_stored, count(16, m, 0))
                    nc.scalar.activation(bc[:, :], ps[0:2 * S, 1, :], ACT.Copy).then_inc(bc_done, 1)
                    nc.scalar.activation(low[:, :], ps[:, 0, :], ACT.Copy).then_inc(low_done, 1)
                if s == 10:
                    act.wait_ge(scan_done, count(S, m, -S))
                    act.wait_ge(bx_done, count(S, m, -S))
                    act.wait_ge(sp_rest, count(1, m, 0))
                    for i in range(2):
                        ps = front_bank(f"dt{i}")
                        act.wait_ge(filled_f, front_use(f"dt{i}", m))
                        for k in range(2):
                            j = 2 * i + k
                            nc.scalar.activation(sp_e[:, j, :], ps[:, k, :], ACT.Abs, bias=pcol(C_DTB + j))
                            last = nc.scalar.activation(dt[:, b, j, :], ps[:, k, :], ACT.Relu, bias=pcol(C_DTB + j))
                        last.then_inc(relu_done, 1)
                if s == 11:
                    act.wait_ge(relu_done, count(2, m, 2))
                    nc.scalar.activation(sp_e[:, :, :], sp_e[:, :, :], ACT.Exp, scale=-1.0).then_inc(sp_exp, 1)
                if s == 12:
                    nc.scalar.preload_act_table_set("natural_log")
                    act.wait_ge(sp_one, count(1, m, 1))
                    nc.scalar.activation(sp_l[:, :, :], sp_l[:, :, :], ACT.Ln).then_inc(sp_ln, 1)
                    use_log_exp()

            def decay(s, n):
                act.wait_ge(scan_done, count(S, n, s + 1 - RA))
                for j in range(NJ):
                    last = nc.scalar.activation(dA[:, s % RA, j, :], dt[:, n[1], j, :], ACT.Exp,
                                                scale=neg_a[:, j, s:s + 1])
                last.then_inc(exp_done, 1)

            def main(s, n):
                if s == 0:
                    act.wait_ge(dt_done, count(1, n, 1))
                    if is_first(n):
                        act.wait_ge(a_ready, 1)
                    decay(0, n)
                if s == 8:
                    use_log_exp()
                if s < S - 1:
                    decay(s + 1, n)

            def back(s, m):
                if s == 0:
                    act.wait_ge(x1x_done, count(1, m, 0))
                    act.dma_start(xb[:, :, :], x_v[m[0], m[1]]).then_inc(xb_loaded, 16)
                if s == 2:
                    inv_std(2, m)
                if s == 3:
                    ps = back_bank("vT")
                    act.wait_ge(filled_b, back_use("vT", m))
                    nc.scalar.activation(vT[:, 0, :], ps[:, 0, :], ACT.Identity, scale=pcol(C_LN2W), bias=pcol(C_LN2B))
                    nc.scalar.activation(vT[:, 1, :], ps[:, 1, :], ACT.Identity, scale=pcol(C_LN2W + 1),
                                         bias=pcol(C_LN2B + 1)).then_inc(vT_done, 1)
                if s == 7:
                    act.wait_ge(filled_b, back_use_before("fo", m))
                    for i in range(2):
                        ps = back_bank(f"G{i}")
                        act.wait_ge(filled_b, back_use(f"G{i}", m))
                        nc.scalar.activation(hg[:, 2 * i:2 * i + 2, :], ps[:, :, :], ACT.Silu).then_inc(gate_done, 1)
                if s == 8 and is_last(m):
                    use_log_exp()
                if s == 9:
                    inv_std(3, m)
                if s == 10:
                    act.wait_ge(nrm_done, count(1, m, 1))
                    nc.scalar.activation(lnn[:, :], nrm[:, 2, :], ACT.Ln, scale=float(2 ** LIFT)).then_inc(lnn_done, 1)
                    act.wait_ge(lnn_done, count(1, m, 1))
                    nc.scalar.activation(rn[:, :], lnn[:, :], ACT.Exp, scale=-0.5, bias=lift_c[:, :]).then_inc(rn_done, 1)
                    ps = back_bank("xeT")
                    act.wait_ge(filled_b, back_use("xeT", m))
                    nc.scalar.activation(xeT[:, :, :], ps[:, :, :], ACT.Copy).then_inc(xeT_done, 1)
                if s == 11:
                    act.wait_ge(lgm_done, count(1, m, 1))
                    nc.scalar.activation(pr[:, :, :], lgm[:, :, :], ACT.Exp).then_inc(pr_done, 1)
                if s == 12:
                    ps = back_bank("cT")
                    act.wait_ge(filled_b, back_use("cT", m))
                    act.wait_ge(cw_stored, count(16, m, 0))
                    nc.scalar.activation(cT[:, :], ps[0:NE].rearrange("p k t -> p (k t)")[:, 0:T], ACT.Copy
                                         ).then_inc(cT_done, 1)

            drive(act, front, main, back)

        @block.vector
        def _(dve):
            nc.vector.memset(eps_c[:, :], EPS).then_inc(consts_ready, 1)
            nc.vector.memset(lift_c[:, :], 0.5 * LIFT * math.log(2.0)).then_inc(consts_ready, 1)
            dve.wait_ge(loaded["par"], 16)
            dve.wait_ge(a_exp, 1)
            nc.vector.tensor_scalar(neg_a[:, :, :], exp_a[:, :, :], -1.0, None, ALU.mult).then_inc(a_ready, 1)
            dve.wait_ge(state_zero, 1)

            links = {"f": 0, "b": 0}

            def link(which, m, ins):
                chain, per = (front_chain, LINKS_FRONT) if which == "f" else (back_chain, LINKS_BACK)
                links[which] = links[which] % per + 1
                ins.then_inc(chain, 1)
                dve.wait_ge(chain, count(per, m, links[which]))

            def norm_stats(k, src, which, m):
                for j in range(SUB):
                    last = nc.vector.bn_stats(bn[k][:, j, :], src[:, j, :])
                link(which, m, last)
                nc.vector.memset(pause[:, :], 0.0)
                for j in range(SUB):
                    last = nc.vector.bn_aggr(mv[k][:, j, :], bn[k][:, j, :])
                last.then_inc(stats[k], 1)

            def normalise(k, dst, src, done, m):
                dve.wait_ge(rstd_done[k], count(1, m, 1))
                for j in range(SUB):
                    last = nc.vector.tensor_scalar(dst[:, j, :], src[:, j, :], mv[k][:, j, 0:1], rstd[k][:, j:j + 1],
                                                   ALU.subtract, ALU.mult)
                last.then_inc(done, 1)

            def front(s, m):
                b = m[1]
                if s == 1:
                    dve.wait_ge(xf_loaded, count(16, m, 16))
                    norm_stats(0, xf, "f", m)
                if s == 2:
                    dve.wait_ge(x1_done, count(1, m, -1))
                    normalise(0, xn[:, b], xf, xn_done, m)
                    dve.wait_ge(xn_done, count(1, m, 1))
                    norm_stats(1, xn[:, b], "f", m)
                if s == 3:
                    dve.wait_ge(filled_f, front_use_before("uT", m))
                    normalise(1, un, xn[:, b], un_done, m)
                if s in (5, 6):
                    if s == 5:
                        dve.wait_ge(xm_done, count(2, m, 2))
                        dve.wait_ge(sp_log, count(1, m, 0))
                    for tap in (2 * (s - 5), 2 * (s - 5) + 1):
                        k = TAPS - 1 - tap
                        for j in range(NJ):
                            done = tap * NJ + j
                            w = pcol(C_CONVW + j * TAPS + k)
                            if tap == 0:
                                ins = nc.vector.tensor_scalar(acc[:, j, :], xm[:, b, j, k:k + T], w,
                                                              pcol(C_CONVB + j), ALU.mult, ALU.add)
                            else:
                                dve.wait_ge(conv_tap, count(NJ * TAPS, m, done - NJ + 1))
                                ins = nc.vector.scalar_tensor_tensor(out=acc[:, j, :], in0=xm[:, b, j, k:k + T],
                                                                     scalar=w, in1=acc[:, j, :],
                                                                     op0=ALU.mult, op1=ALU.add)
                            ins.then_inc(conv_tap, 1)
                if s == 11:
                    dve.wait_ge(sp_exp, count(1, m, 1))
                    nc.vector.tensor_scalar(sp_l[:, :, :], sp_e[:, :, :], 1.0, None, ALU.add).then_inc(sp_one, 1)
                    dve.wait_ge(xc_done, count(1, m, 1))
                    nc.vector.tensor_scalar(acc[:, :, :], sp_e[:, :, :], 1.0, -1.0, ALU.add, ALU.add
                                            ).then_inc(sp_back, 1)
                if s == 12:
                    dve.wait_ge(sp_ln, count(1, m, 1))
                    dve.wait_ge(sp_back, count(1, m, 1))
                    nc.vector.scalar_tensor_tensor(out=sp_l[:, :, :], in0=acc[:, :, :], scalar=0.0, in1=sp_l[:, :, :],
                                                   op0=ALU.is_gt, op1=ALU.mult).then_inc(sp_masked, 1)
                if s == 14:
                    dve.wait_ge(sp_log, count(1, m, 1))
                    nc.vector.tensor_tensor(dt[:, b], dt[:, b], sp_l[:, :, :], ALU.add).then_inc(dt_done, 1)
                    dve.wait_ge(dt_done, count(1, m, 1))
                    link("f", m, nc.vector.tensor_tensor(u[:, b], dt[:, b], xc[:, b], ALU.mult))

            def product(s, n):
                b, r, g = n[1], s % RB, s // G
                if s % G == 0:
                    dve.wait_ge(b_loaded[g % RINGG], count(16 * NG // RINGG, n, 16 * (g // RINGG + 1)))
                dve.wait_ge(scan_done, count(S, n, s + 1 - RB))
                nc.vector.tensor_tensor(bx[:, r], u[:, b],
                                        bB[:, g % RINGG, s % G:s % G + 1, :].to_broadcast([P, NJ, T]),
                                        ALU.mult).then_inc(bx_done, 1)

            def main(s, n):
                b, r = n[1], s % RB
                if s == 0:
                    product(0, n)
                if s < S - 1:
                    product(s + 1, n)
                dve.wait_ge(bx_done, count(S, n, s + 1))
                dve.wait_ge(exp_done, count(S, n, s + 1))
                dve.wait_ge(hc_done, count(S, n, s + 1 - RB))
                dve.wait_ge(state_saved, count(S, n, s + 1 - RB))
                for j in range(NJ):
                    last = nc.vector.tensor_tensor_scan(h[:, r, j, :], dA[:, s % RA, j, :], bx[:, r, j, :],
                                                        state[:, b, j, s:s + 1], ALU.mult, ALU.add)
                last.then_inc(scan_done, 1)

            def finish(m):
                ps = back_bank("wb")
                dve.wait_ge(filled_b, back_use("wb", m))
                dve.wait_ge(out_stored, count(16, m, 0))
                nc.vector.tensor_tensor(fin[:, :, :], x2[:, :, :], ps[:, :, :], ALU.add).then_inc(fin_done, 1)

            def back(s, m):
                b = m[1]
                if s == 0:
                    dve.wait_ge(y_summed, count(S, m, S))
                    dve.wait_ge(filled_b, back_use_before("op", m))
                    for j in range(NJ):
                        last = nc.vector.scalar_tensor_tensor(out=yg[:, j, :], in0=xc[:, b, j, :],
                                                              scalar=pcol(C_DSKIP + j), in1=psy[j // 2][:, j % 2, :],
                                                              op0=ALU.mult, op1=ALU.add)
                    last.then_inc(y_skip, 1)
                    if not is_first(m):
                        finish(prev(m))
                if s == 2:
                    ps = back_bank("op")
                    dve.wait_ge(filled_b, back_use("op", m))
                    dve.wait_ge(x1x_done, count(1, m, 0))
                    nc.vector.tensor_tensor(x1[:, :, :], xn[:, b], ps[:, :, :], ALU.add).then_inc(x1_done, 1)
                    dve.wait_ge(x1_done, count(1, m, 1))
                    norm_stats(2, x1, "b", m)
                if s == 3:
                    dve.wait_ge(filled_b, back_use_before("vT", m))
                    normalise(2, vn, x1, vn_done, m)
                if s in (7, 8):
                    i = s - 7
                    dve.wait_ge(gate_done, count(2, m, i + 1))
                    ps = back_bank(f"A{i}")
                    dve.wait_ge(filled_b, back_use(f"A{i}", m))
                    nc.vector.tensor_tensor(hg[:, 2 * i:2 * i + 2, :], hg[:, 2 * i:2 * i + 2, :], ps[:, :, :], ALU.mult
                                            ).then_inc(hg_done, 1)
                if s == 9:
                    ps = back_bank("fo")
                    dve.wait_ge(filled_b, back_use("fo", m))
                    dve.wait_ge(x1x_done, count(1, m, 1))
                    dve.wait_ge(fin_done, count(1, m, 0))
                    nc.vector.tensor_tensor(x2[:, :, :], x1x[:, :, :], ps[:, :, :], ALU.add).then_inc(x2_done, 1)
                    dve.wait_ge(x2_done, count(1, m, 1))
                    norm_stats(3, x2, "b", m)
                if s == 10:
                    dve.wait_ge(filled_b, back_use_before("xeT", m))
                    normalise(3, xe, x2, xe_done, m)
                    var = mv[3][:, :, 1]
                    link("b", m, nc.vector.scalar_tensor_tensor(out=nrm[:, 0, :], in0=var, scalar=float(DM),
                                                                in1=rstd[3][:, :], op0=ALU.mult, op1=ALU.mult))
                    link("b", m, nc.vector.tensor_tensor(nrm[:, 1, :], nrm[:, 0, :], rstd[3][:, :], ALU.mult))
                    nc.vector.tensor_scalar(nrm[:, 2, :], nrm[:, 1, :], NORM_FLOOR * NORM_FLOOR, None, ALU.max
                                            ).then_inc(nrm_done, 1)
                if s == 11:
                    ps = back_bank("rt")
                    dve.wait_ge(filled_b, back_use("rt", m))
                    dve.wait_ge(rn_done, count(1, m, 1))
                    for j in range(SUB):
                        last = nc.vector.tensor_scalar(lg[:, j, :], ps[:, 0, j * NE:(j + 1) * NE], rn[:, j:j + 1], None,
                                                       ALU.mult)
                    link("b", m, last)
                    link("b", m, nc.vector.reduce_max(mx[:, :], lg[:, :, :], X))
                    nc.vector.tensor_tensor(lgm[:, :, :], lg[:, :, :], mx[:, :].unsqueeze(2).to_broadcast([P, SUB, NE]),
                                            ALU.subtract).then_inc(lgm_done, 1)
                    dve.wait_ge(pr_done, count(1, m, 1))
                    p_j = pr[:, :, :].unsqueeze(2).to_broadcast([P, SUB, NE, NE])
                    p_e = pr[:, :, :].unsqueeze(3).to_broadcast([P, SUB, NE, NE])
                    nc.vector.tensor_tensor(gt[:, :, :, :], p_j, p_e, ALU.is_gt)
                    link("b", m, nc.vector.tensor_tensor(eq[:, :, :, :], p_j, p_e, ALU.is_equal))
                    if is_first(m):
                        dve.wait_ge(earlier_ready, 1)
                    link("b", m, nc.vector.tensor_tensor(eq[:, :, :, :], eq[:, :, :, :],
                                                         earlier[:, :, :].unsqueeze(1).to_broadcast([P, SUB, NE, NE]),
                                                         ALU.mult))
                    link("b", m, nc.vector.tensor_tensor(gt[:, :, :, :], gt[:, :, :, :], eq[:, :, :, :], ALU.add))
                    link("b", m, nc.vector.reduce_sum(rank[:, :, :], gt[:, :, :, :], X))
                    link("b", m, nc.vector.scalar_tensor_tensor(out=psel[:, :, :], in0=rank[:, :, :], scalar=1.5,
                                                                in1=pr[:, :, :], op0=ALU.is_lt, op1=ALU.mult))
                    link("b", m, nc.vector.reduce_sum(den[:, :], psel[:, :, :], X))
                    link("b", m, nc.vector.reciprocal(rden[:, :], den[:, :]))
                    dve.wait_ge(filled_b, back_use_before("cT", m))
                    nc.vector.tensor_tensor(cw[:, :, :], psel[:, :, :], rden[:, :].unsqueeze(2).to_broadcast([P, SUB, NE]),
                                            ALU.mult).then_inc(cw_done, 1)
                if s in (13, 14):
                    for i in (2 * (s - 13), 2 * (s - 13) + 1):
                        ps = back_bank(f"wa{i}")
                        dve.wait_ge(filled_b, back_use(f"wa{i}", m))
                        if i == 0:
                            dve.wait_ge(cbc_loaded, count(16, m, 16))
                        nc.vector.tensor_tensor(cbc[:, 2 * i:2 * i + 2, :], cbc[:, 2 * i:2 * i + 2, :], ps[:, :, :],
                                                ALU.mult).then_inc(hE_done, 1)

            drive(dve, front, main, back)
            finish((NC - 1, B - 1))

        @block.tensor
        def _(pe):
            mm = nc.tensor.matmul
            pe.wait_ge(ident_ready, 1)

            def transposes(dst, src):
                for k in range(KM):
                    for j in range(SUB):
                        last = nc.tensor.transpose(dst[:, k, j * P:(j + 1) * P], src[:, j, k * P:(k + 1) * P], ident[:, :])
                return last

            def project(dst, w, rhs, kt, cols):
                for i, c in enumerate(cols):
                    for k in range(kt):
                        last = mm(dst[:, i, :], w[:, k, c:c + P], rhs[:, k, :], start=k == 0, stop=k == kt - 1)
                return last

            def project_tokens(dst, lhs, w, kt):
                for j in range(SUB):
                    for k in range(kt):
                        last = mm(dst[:, j, :], lhs[:, k, j * P:(j + 1) * P], w[:, k, :], start=k == 0, stop=k == kt - 1)
                return last

            def first(m, key):
                if is_first(m):
                    pe.wait_ge(loaded[key], 16)

            def front(s, m):
                b = m[1]
                if s == 3:
                    ps = front_bank("uT")
                    pe.wait_ge(relu_done, count(2, m, -1))
                    pe.wait_ge(un_done, count(1, m, 1))
                    transposes(ps, un).then_inc(filled_f, 1)
                if s == 4:
                    first(m, "in")
                    pe.wait_ge(relu_done, count(2, m, 0))
                    pe.wait_ge(low_done, count(1, m, 0))
                    pe.wait_ge(uT_done, count(1, m, 1))
                    for i in range(2):
                        project(front_bank(f"x{i}"), w_in_sb, uT, KM, [(2 * i + k) * P for k in range(2)]
                                ).then_inc(filled_f, 1)
                if s == 5:
                    project(front_bank("z0"), w_in_sb, uT, KM, [DI, DI + P]).then_inc(filled_f, 1)
                if s == 6:
                    pe.wait_ge(xm_done, count(2, m, 1))
                    project(front_bank("z1"), w_in_sb, uT, KM, [DI + 2 * P, DI + 3 * P]).then_inc(filled_f, 1)
                if s == 9:
                    first(m, "x")
                    pe.wait_ge(xc_done, count(1, m, 1))
                    ps = front_bank("low")
                    pe.wait_ge(xm_done, count(2, m, 2))
                    for k in range(NJ):
                        mm(ps[0:2 * S, 1, :], w_x_sb[:, k, DTR:DTR + 2 * S], xc[:, b, k, :], start=k == 0, stop=k == NJ - 1)
                    for k in range(NJ):
                        last = mm(ps[:, 0, :], w_x_sb[:, k, 0:DTR], xc[:, b, k, :], start=k == 0, stop=k == NJ - 1)
                    last.then_inc(filled_f, 1)
                if s == 10:
                    first(m, "dt")
                    pe.wait_ge(low_done, count(1, m, 1))
                    for i in range(2):
                        ps = front_bank(f"dt{i}")
                        pe.wait_ge(sz_done, count(2, m, i + 1))
                        for k in range(2):
                            j = 2 * i + k
                            last = mm(ps[:, k, :], w_dt_sb[:, j * P:(j + 1) * P], low[:, :], start=True, stop=True)
                        last.then_inc(filled_f, 1)

            def sum_states(s, n):
                r = s % RB
                pe.wait_ge(hc_done, count(S, n, s + 1))
                if s == 0:
                    pe.wait_ge(y_skip, count(1, n, 0))
                for i in range(2):
                    last = mm(psy[i][:, :, :], ident[:, :], hC[:, r, 2 * i:2 * i + 2, :], start=s == 0, stop=s == S - 1)
                last.then_inc(y_summed, 1)

            def main(s, n):
                if s > 0:
                    sum_states(s - 1, n)

            def back(s, m):
                if s == 0:
                    sum_states(S - 1, m)
                if s == 1:
                    first(m, "out")
                    pe.wait_ge(hE_done, count(NE // 2, m, -1))
                    pe.wait_ge(yg_done, count(1, m, 1))
                    project_tokens(back_bank("op"), yg, w_out_sb, NJ).then_inc(filled_b, 1)
                if s == 3:
                    pe.wait_ge(hE_done, count(NE // 2, m, 0))
                    pe.wait_ge(vn_done, count(1, m, 1))
                    transposes(back_bank("vT"), vn).then_inc(filled_b, 1)
                if s == 4:
                    first(m, "ff")
                    pe.wait_ge(fin_done, count(1, m, 0))
                    pe.wait_ge(vT_done, count(1, m, 1))
                    project(back_bank("G0"), w_ff_sb, vT, KM, [HID // 2, HID // 2 + P]).then_inc(filled_b, 1)
                if s == 5:
                    pe.wait_ge(x1_done, count(1, m, 1))
                    project(back_bank("G1"), w_ff_sb, vT, KM, [HID // 2 + 2 * P, HID // 2 + 3 * P]).then_inc(filled_b, 1)
                if s == 6:
                    project(back_bank("A0"), w_ff_sb, vT, KM, [0, P]).then_inc(filled_b, 1)
                if s == 7:
                    pe.wait_ge(gate_done, count(2, m, 1))
                    project(back_bank("A1"), w_ff_sb, vT, KM, [2 * P, 3 * P]).then_inc(filled_b, 1)
                if s == 8:
                    first(m, "fo")
                    pe.wait_ge(gate_done, count(2, m, 2))
                    pe.wait_ge(hg_done, count(2, m, 2))
                    project_tokens(back_bank("fo"), hg, w_fo_sb, F1).then_inc(filled_b, 1)
                if s == 10:
                    pe.wait_ge(xe_done, count(1, m, 1))
                    transposes(back_bank("xeT"), xe).then_inc(filled_b, 1)
                    first(m, "r")
                    pe.wait_ge(xeT_done, count(1, m, 1))
                    ps = back_bank("rt")
                    for j in range(SUB):
                        for k in range(KM):
                            last = mm(ps[:, 0, j * NE:(j + 1) * NE], xeT[:, k, j * P:(j + 1) * P], w_r_sb[:, k, :],
                                      start=k == 0, stop=k == KM - 1)
                    last.then_inc(filled_b, 1)
                if s == 11:
                    pe.wait_ge(x2_done, count(1, m, 1))
                    pe.wait_ge(cw_done, count(1, m, 1))
                    ps = back_bank("cT")
                    for j in range(SUB):
                        last = nc.tensor.transpose(ps[0:NE, 0, j * P:(j + 1) * P], cw[:, j, :], ident[:, :])
                    last.then_inc(filled_b, 1)
                if s in (12, 13):
                    first(m, "a")
                    for i in (2 * (s - 12), 2 * (s - 12) + 1):
                        if i == 2:
                            pe.wait_ge(cT_done, count(1, m, 1))
                        if i == 3:
                            pe.wait_ge(hE_done, count(NE // 2, m, 1))
                        project(back_bank(f"wa{i}"), w_a_sb, xeT, KM, [2 * i * RANK, (2 * i + 1) * RANK]
                                ).then_inc(filled_b, 1)
                if s == 15:
                    first(m, "b")
                    pe.wait_ge(hE_done, count(NE // 2, m, NE // 2))
                    project_tokens(back_bank("wb"), cbc, w_b_sb, NE).then_inc(filled_b, 1)

            drive(pe, front, main, back)


def kernel(**inputs):
    import numpy as np
    import concourse.bacc as bacc
    from concourse.bass_utils import run_bass_kernel_spmd

    def get(name):
        return np.asarray(inputs[name])

    def tiles(w):
        k, m = w.shape
        return np.ascontiguousarray(w.reshape(k // P, P, m).transpose(1, 0, 2).reshape(P, -1))

    def columns(v):
        return tiles(v.reshape(v.shape[0], -1))

    params = np.ascontiguousarray(np.concatenate([
        columns(get("L0_attn_conv_w")), columns(get("L0_attn_conv_b")), columns(get("L0_attn_dt_proj_b")),
        columns(get("L0_attn_D_skip")), columns(get("L0_attn_A_log")),
        columns(get("L0_attn_ln1_w")), columns(get("L0_attn_ln1_b")),
        columns(get("L0_attn_ln2_w")), columns(get("L0_attn_ln2_b"))], axis=1))
    arrays = {
        "x": np.ascontiguousarray(get("L0_attn_x")),
        "params": params,
        "w_in": tiles(get("L0_attn_in_proj_w").T),
        "w_x": tiles(get("L0_attn_x_proj_w").T),
        "w_dt": tiles(get("L0_attn_dt_proj_w").T),
        "w_out": tiles(get("L0_attn_out_proj_w").T),
        "w_ff": tiles(get("L0_attn_ff_proj_w").T),
        "w_fo": tiles(get("L0_attn_ff_out_w").T),
        "w_a": tiles(get("L0_ffn_Wa").transpose(1, 0, 2).reshape(DM, NE * RANK)),
        "w_b": tiles(get("L0_ffn_Wb").reshape(NE * RANK, DM)),
        "w_r": tiles(get("L0_ffn_router_w")),
    }
    f32 = mybir.dt.float32
    nc = bacc.Bacc("TRN2", target_bir_lowering=False, num_devices=1)
    aps = {k: nc.dram_tensor(f"in_{k}", a.shape, f32, kind="ExternalInput").ap() for k, a in arrays.items()}
    bc_scratch = nc.dram_tensor("bc_scratch", (2 * S, T), f32, kind="Internal").ap()
    cw_scratch = nc.dram_tensor("cw_scratch", (NE, T), f32, kind="Internal").ap()
    out = nc.dram_tensor("out_0", (B, L, DM), f32, kind="ExternalOutput").ap()
    mamba_moe(nc, aps["x"], aps["params"], aps["w_in"], aps["w_x"], aps["w_dt"], aps["w_out"], aps["w_ff"],
              aps["w_fo"], aps["w_a"], aps["w_b"], aps["w_r"], bc_scratch, cw_scratch, out)
    r = run_bass_kernel_spmd(nc, [{f"in_{k}": a for k, a in arrays.items()}], core_ids=[0])
    return r.results[0]["out_0"]
```

```python
import math
from contextlib import ExitStack

import concourse.bass as bass
from concourse import mybir

B, L, DM, DI, S, TAPS, DTR, HID = 2, 2048, 256, 512, 16, 4, 128, 1024
NE, RANK = 8, 128
P = 128
T = 256
SUB = T // P
KM = DM // P
NJ = DI // P
NC = L // T
G = 4
NG = S // G
RINGG = 2
RB = 2
RC = 4
RA = 4

AHEAD = 2
CONV = 6
WB_SLOTS = (2, 3)
FIN_SLOT = 5
WEIGH = {0: (0, 1), 1: (2,), 2: (3,)}
DT_SLOT = 13
SP_SLOT = 12
ADDED = (1, 4, 7, 9)
POOL_PRODUCTS = (1, 3, 7, 8)
F1 = HID // 2 // P
EPS = 1e-5
NORM_FLOOR = 1e-12
LIFT = 20

C_CONVW, C_CONVB, C_DTB, C_DSKIP, C_ALOG = 0, NJ * TAPS, NJ * TAPS + NJ, NJ * TAPS + 2 * NJ, NJ * TAPS + 3 * NJ
C_LN1W = C_ALOG + NJ * S
C_LN1B, C_LN2W, C_LN2B = C_LN1W + KM, C_LN1W + 2 * KM, C_LN1W + 3 * KM
NPAR = C_LN1W + 4 * KM

FRONT_UNITS = ["uT", "x0", "x1", "low", "bc", "dt0", "dt1", "z0", "z1"]
BACK_UNITS = ["op", "vT", "G0", "G1", "A0", "A1", "fo", "xeT", "rt", "wa0", "wa1", "cT", "wa2", "wa3"]
BACK_BANKS = [0, 1] + [i % 3 for i in range(len(BACK_UNITS) - 2)]
RING = 3
WB_BANK = 2

LINKS_FRONT = 2
LINKS_BACK = 2 + 2 + 9


def count(per_step, step, k):
    c, b = step
    value = c * (2 * per_step) + (per_step * b + k)
    return max(value, 0) if isinstance(value, int) else value


TAIL = FIN_SLOT + 1


def is_first(step):
    return isinstance(step[0], int) and step == (0, 0)


def is_last(step):
    return isinstance(step[0], int) and step == (NC - 1, B - 1)


def prev(step):
    c, b = step
    return (c, 0) if b else (c - 1, 1)


def products(engine, k):
    on_pool = sum(s < k for s in POOL_PRODUCTS)
    return on_pool if engine == "pool" else k - on_pool


def sums(k):
    return k - sum(s < k for s in ADDED)


def following(step):
    c, b = step
    return (c + 1, 0) if b else (c, 1)


def drive(eng, front, main, back, tail):
    def step(before, now, after):
        for s in range(S):
            if now:
                main(s, now)
            if before and not is_first(before):
                tail(s, prev(before))
            if before:
                back(s, before)
            if after:
                front(s, after)

    step(None, None, (0, 0))
    step(None, (0, 0), (0, 1))
    step((0, 0), (0, 1), (1, 0))
    with eng.Fori(1, NC - 1) as c:
        step((c - 1, 1), (c, 0), (c, 1))
        step((c, 0), (c, 1), (c + 1, 0))
    step((NC - 2, 1), (NC - 1, 0), (NC - 1, 1))
    step((NC - 1, 0), (NC - 1, 1), None)
    step((NC - 1, 1), None, None)
    for s in range(TAIL):
        tail(s, (NC - 1, 1))


def mamba_moe(nc, x, params, w_in, w_x, w_dt, w_out, w_ff, w_fo, w_a, w_b, w_r, bc_scratch, cw_scratch, out):
    f32 = mybir.dt.float32
    ALU = mybir.AluOpType
    ACT = mybir.ActivationFunctionType
    X = mybir.AxisListType.X

    x_v = x.rearrange("b (c j p) d -> c b p j d", p=P, j=SUB)
    out_v = out.rearrange("b (c j p) d -> c b p j d", p=P, j=SUB)

    ctx = ExitStack()
    with ctx:
        def sb(name, shape):
            return ctx.enter_context(nc.sbuf_tensor(name, shape, f32))

        def sem(name):
            return ctx.enter_context(nc.semaphore(name))

        par = sb("par", [P, NPAR])
        w_in_sb = sb("w_in_sb", [P, KM, 2 * DI])
        w_x_sb = sb("w_x_sb", [P, NJ, DTR + 2 * S])
        w_dt_sb = sb("w_dt_sb", [P, DI])
        w_out_sb = sb("w_out_sb", [P, NJ, DM])
        w_ff_sb = sb("w_ff_sb", [P, KM, HID])
        w_fo_sb = sb("w_fo_sb", [P, F1, DM])
        w_a_sb = sb("w_a_sb", [P, KM, NE * RANK])
        w_b_sb = sb("w_b_sb", [P, NE, DM])
        w_r_sb = sb("w_r_sb", [P, KM, NE])
        ident = sb("ident", [P, P])
        earlier = sb("earlier", [P, NE, NE])
        neg_a = sb("neg_a", [P, NJ, S])
        exp_a = sb("exp_a", [P, NJ, S])
        eps_c = sb("eps_c", [P, 1])
        lift_c = sb("lift_c", [P, 1])
        one_c = sb("one_c", [P, 1])
        ln_one = sb("ln_one", [P, 1])

        xf = sb("xf", [P, SUB, DM])
        xn = sb("xn", [P, B, SUB, DM])
        un = sb("un", [P, SUB, DM])
        uT = sb("uT", [P, KM, T])
        xm = sb("xm", [P, B, NJ, TAPS - 1 + T])
        acc = sb("acc", [P, NJ, T])
        xc = sb("xc", [P, B, NJ, T])
        sz = sb("sz", [P, B, NJ, T])
        low = sb("low", [P, T])
        bc = sb("bc", [2 * S, T])
        sp_e = sb("sp_e", [P, NJ, T])
        sp_l = sb("sp_l", [P, NJ, T])
        dt = sb("dt", [P, B, NJ, T])
        u = sb("u", [P, B, NJ, T])
        bn = [sb(f"bn{k}", [P, SUB, 6]) for k in range(4)]
        mv = [sb(f"mv{k}", [P, SUB, 2]) for k in range(4)]
        lnv = [sb(f"lnv{k}", [P, SUB]) for k in range(4)]
        rstd = [sb(f"rstd{k}", [P, SUB]) for k in range(4)]

        pause = sb("pause", [P, 1])

        bB = sb("bB", [P, RINGG, G, T])
        bC = sb("bC", [P, RINGG, G, T])
        dA = sb("dA", [P, RA, NJ, T])
        bx = sb("bx", [P, RB, NJ, T])
        h = sb("h", [P, RB, NJ, T])
        hC = sb("hC", [P, RC, NJ, T])
        state = sb("state", [P, B, NJ, S])

        xb = sb("xb", [P, SUB, DM])
        yg = sb("yg", [P, NJ, T])
        x1 = sb("x1", [P, SUB, DM])
        nx = sb("nx", [P, SUB, DM])
        nT = sb("nT", [P, KM, T])
        hg = sb("hg", [P, F1, T])
        x2 = sb("x2", [P, SUB, DM])
        nrm = sb("nrm", [P, 3, SUB])
        lnn = sb("lnn", [P, SUB])
        rn = sb("rn", [P, SUB])
        lg = sb("lg", [P, SUB, NE])
        lgm = sb("lgm", [P, SUB, NE])
        mx = sb("mx", [P, SUB])
        pr = sb("pr", [P, SUB, NE])
        gt = sb("gt", [P, SUB, NE, NE])
        eq = sb("eq", [P, SUB, NE, NE])
        rank = sb("rank", [P, SUB, NE])
        psel = sb("psel", [P, SUB, NE])
        den = sb("den", [P, SUB])
        rden = sb("rden", [P, SUB])
        cw = sb("cw", [P, SUB, NE])
        cT = sb("cT", [NE, T])
        cbc = sb("cbc", [P, NE, T])

        psy = [ctx.enter_context(nc.psum_tensor(f"psy{i}", [P, 2, T], f32)) for i in range(2)]
        psf = [ctx.enter_context(nc.psum_tensor(f"psf{i}", [P, 2, T], f32)) for i in range(RING)]
        psb = [ctx.enter_context(nc.psum_tensor(f"psb{i}", [P, 2, T], f32)) for i in range(RING)]

        loaded = {k: sem(f"loaded_{k}") for k in ("par", "in", "x", "dt", "out", "ff", "fo", "a", "b", "r")}
        ident_zero, ident_ready = sem("ident_zero"), sem("ident_ready")
        earlier_one, earlier_ready = sem("earlier_one"), sem("earlier_ready")
        consts_ready, state_zero, halo_zero = sem("consts_ready"), sem("state_zero"), sem("halo_zero")
        a_exp, a_ready = sem("a_exp"), sem("a_ready")
        filled_f, filled_b = sem("filled_f"), sem("filled_b")
        wb_filled = sem("wb_filled")
        xf_loaded, xb_loaded = sem("xf_loaded"), sem("xb_loaded")
        stats = [sem(f"stats{k}") for k in range(4)]
        lnv_done = [sem(f"lnv_done{k}") for k in range(4)]
        rstd_done = [sem(f"rstd_done{k}") for k in range(4)]
        xn_done, un_done, uT_done = sem("xn_done"), sem("un_done"), sem("uT_done")
        halo_moved, xm_done = sem("halo_moved"), sem("xm_done")
        tap0_done, conv_tap = sem("tap0_done"), sem("conv_tap")
        z_copied, sz_done, xc_done = sem("z_copied"), sem("sz_done"), sem("xc_done")
        low_done, bc_done = sem("low_done"), sem("bc_done")
        bc_stored = sem("bc_stored")
        b_loaded = [sem(f"b_loaded{i}") for i in range(RINGG)]
        c_loaded = [sem(f"c_loaded{i}") for i in range(RINGG)]
        relu_done, sp_exp, sp_ln = sem("relu_done"), sem("sp_exp"), sem("sp_ln")
        ln_one_ready = sem("ln_one_ready")
        sp_back, sp_rest, sp_added = sem("sp_back"), sem("sp_rest"), sem("sp_added")
        dt_done, u_done = sem("dt_done"), sem("u_done")
        exp_done, scan_done = sem("exp_done"), sem("scan_done")
        bx_done = {"dve": sem("bx_dve_done"), "pool": sem("bx_pool_done")}
        hc_done, state_saved = sem("hc_done"), sem("state_saved")
        pair_added, y_summed = sem("pair_added"), sem("y_summed")
        y_skip, yg_done = sem("y_skip"), sem("yg_done")
        xn_copied = sem("xn_copied")
        x1_done, x1x_done = sem("x1_done"), sem("x1x_done")
        vn_done, vT_done = sem("vn_done"), sem("vT_done")
        gate_done, hg_done = sem("gate_done"), sem("hg_done")
        x2_done, xe_done, xeT_done = sem("x2_done"), sem("xe_done"), sem("xeT_done")
        nrm_done, lnn_done, rn_done = sem("nrm_done"), sem("lnn_done"), sem("rn_done")
        lgm_done, pr_done, cw_done, cT_done = sem("lgm_done"), sem("pr_done"), sem("cw_done"), sem("cT_done")
        cw_stored, cbc_loaded = sem("cw_stored"), sem("cbc_loaded")
        hE_done, fin_done, out_stored = sem("hE_done"), sem("fin_done"), sem("out_stored")
        front_chain, back_chain = sem("front_chain"), sem("back_chain")

        def pcol(col):
            return par[:, col:col + 1]

        def front_bank(name):
            return psf[FRONT_UNITS.index(name) % RING]

        def back_bank(name):
            return psb[BACK_BANKS[BACK_UNITS.index(name)]]

        def front_use(name, m):
            return count(len(FRONT_UNITS), m, FRONT_UNITS.index(name) + 1)

        def back_use(name, m):
            return count(len(BACK_UNITS), m, BACK_UNITS.index(name) + 1)

        def front_use_before(name, m):
            return count(len(FRONT_UNITS), m, FRONT_UNITS.index(name) + 1 - len(FRONT_UNITS))

        def back_use_before(name, m):
            return count(len(BACK_UNITS), m, BACK_UNITS.index(name) + 1 - len(BACK_UNITS))

        def products_done(engine, m, k):
            turns, k = divmod(k, S)
            return count(products(engine, S), m, turns * products(engine, S) + products(engine, k))

        def sums_done(m, k):
            turns, k = divmod(k, S)
            return count(sums(S), m, turns * sums(S) + sums(k))

        block = ctx.enter_context(nc.Block())

        @block.sync
        def _(sp):
            def flat(w):
                return w[:, :, :].rearrange("p k m -> p (k m)") if len(w.shape) == 3 else w[:, :]

            sp.dma_start(par[:, :], params).then_inc(loaded["par"], 16)

            for key, dst, src in (("in", w_in_sb, w_in), ("x", w_x_sb, w_x), ("dt", w_dt_sb, w_dt)):
                sp.dma_start(flat(dst), src).then_inc(loaded[key], 16)
            late = [("out", w_out_sb, w_out), ("ff", w_ff_sb, w_ff), ("fo", w_fo_sb, w_fo), ("r", w_r_sb, w_r),
                    ("a", w_a_sb, w_a), ("b", w_b_sb, w_b)]

            def store_out(m):
                sp.wait_ge(fin_done, count(1, m, 1))
                sp.dma_start(out_v[m[0], m[1]], x2[:, :, :]).then_inc(out_stored, 16)

            def value(v):
                if not isinstance(v, int):
                    sp.compute_val(v)
                return v

            def readers(m, g):
                k = G * (g - RINGG + 1)
                return (value(products_done("dve", m, k)), value(products_done("pool", m, k)), value(count(S, m, k)))

            def load_group(m, g, read):
                by_dve, by_pool, by_hc = read
                sp.wait_ge(bx_done["dve"], by_dve)
                sp.wait_ge(bx_done["pool"], by_pool)
                sp.dma_start(bB[:, g % RINGG], bc_scratch[g * G:(g + 1) * G, :].partition_broadcast(P)
                             ).then_inc(b_loaded[g % RINGG], 16)
                sp.wait_ge(hc_done, by_hc)
                sp.dma_start(bC[:, g % RINGG], bc_scratch[S + g * G:S + (g + 1) * G, :].partition_broadcast(P)
                             ).then_inc(c_loaded[g % RINGG], 16)

            def front(s, m):
                if s == 10:
                    spread, read = value(count(16 * NG // RINGG, m, 0)), value(count(1, m, 1))
                    for i in range(RINGG):
                        sp.wait_ge(b_loaded[i], spread)
                        sp.wait_ge(c_loaded[i], spread)
                    sp.wait_ge(bc_done, read)
                    sp.dma_start(bc_scratch, bc[:, :]).then_inc(bc_stored, 16)
                if s == 11:
                    stored, read = value(count(16, m, 16)), readers(m, 0)
                    sp.wait_ge(bc_stored, stored)
                    load_group(m, 0, read)
                if s == 15 and is_first(m):
                    for key, dst, src in late:
                        sp.dma_start(flat(dst), src).then_inc(loaded[key], 16)

            def main(s, n):
                if s in (0, 4, 8):
                    load_group(n, 1 + s // 4, readers(n, 1 + s // 4))

            def tail(s, m):
                if s == FIN_SLOT:
                    store_out(m)

            def back(s, m):
                if s == 13:
                    before, ready = value(count(16, m, 0)), value(count(1, m, 1))
                    stored, used = value(count(16, m, 16)), value(count(1, m, 0))
                    sp.wait_ge(cbc_loaded, before)
                    sp.wait_ge(cT_done, ready)
                    sp.dma_start(cw_scratch, cT[:, :]).then_inc(cw_stored, 16)
                    sp.wait_ge(cw_stored, stored)
                    sp.wait_ge(wb_filled, used)
                    sp.dma_start(cbc[:, :, :], cw_scratch.partition_broadcast(P)).then_inc(cbc_loaded, 16)

            drive(sp, front, main, back, tail)
            sp.wait_ge(out_stored, 16 * B * NC)

        @block.gpsimd
        def _(pool):
            nc.gpsimd.memset(ident[:, :], 0.0).then_inc(ident_zero, 1)
            pool.wait_ge(ident_zero, 1)
            nc.gpsimd.affine_select(out=ident[:, :], in_=ident[:, :], compare_op=ALU.not_equal, fill=1.0,
                                    base=0, pattern=[[-1, P]], channel_multiplier=1).then_inc(ident_ready, 1)
            nc.gpsimd.memset(earlier[:, :, :], 1.0).then_inc(earlier_one, 1)
            pool.wait_ge(earlier_one, 1)
            nc.gpsimd.affine_select(out=earlier[:, :, :], in_=earlier[:, :, :], compare_op=ALU.is_gt, fill=0.0,
                                    base=0, pattern=[[1, NE], [-1, NE]], channel_multiplier=0
                                    ).then_inc(earlier_ready, 1)
            nc.gpsimd.memset(state[:, :, :, :], 0.0).then_inc(state_zero, 1)
            nc.gpsimd.memset(xm[:, :, :, :], 0.0).then_inc(halo_zero, 1)
            pool.wait_ge(state_zero, 1)
            pool.wait_ge(halo_zero, 1)

            def front(s, m):
                b = m[1]
                if s == SP_SLOT:
                    pool.wait_ge(sp_back, count(1, m, 1))
                    pool.wait_ge(sp_ln, count(1, m, 1))
                    nc.gpsimd.tensor_tensor(sp_e[:, :, :], sp_e[:, :, :], acc[:, :, :], ALU.subtract
                                            ).then_inc(sp_rest, 1)
                    pool.wait_ge(sp_rest, count(1, m, 1))
                    nc.gpsimd.tensor_tensor(dt[:, b], dt[:, b], sp_e[:, :, :], ALU.add).then_inc(sp_added, 1)
                if s == 13:
                    pool.wait_ge(dt_done, count(1, m, 1))
                    nc.gpsimd.tensor_tensor(u[:, b], dt[:, b], xc[:, b], ALU.mult).then_inc(u_done, 1)

            def product(s, n):
                r, g = s % RB, s // G
                if s == POOL_PRODUCTS[0]:
                    pool.wait_ge(u_done, count(1, n, 1))
                pool.wait_ge(b_loaded[g % RINGG], count(16 * NG // RINGG, n, 16 * (g // RINGG + 1)))
                pool.wait_ge(scan_done, count(S, n, s + 1 - RB))
                nc.gpsimd.tensor_tensor(bx[:, r], u[:, n[1]],
                                        bB[:, g % RINGG, s % G:s % G + 1, :].to_broadcast([P, NJ, T]),
                                        ALU.mult).then_inc(bx_done["pool"], 1)

            def main(s, n):
                b, r, g = n[1], s % RB, s // G
                if s + 1 in POOL_PRODUCTS:
                    product(s + 1, n)
                pool.wait_ge(scan_done, count(S, n, s + 1))
                if s % G == 0:
                    pool.wait_ge(c_loaded[g % RINGG], count(16 * NG // RINGG, n, 16 * (g // RINGG + 1)))
                pool.wait_ge(y_summed, sums_done(n, s + 1 - RC))
                nc.gpsimd.tensor_tensor(hC[:, s % RC], h[:, r],
                                        bC[:, g % RINGG, s % G:s % G + 1, :].to_broadcast([P, NJ, T]),
                                        ALU.mult).then_inc(hc_done, 1)
                if s - 1 in ADDED:
                    pool.wait_ge(hc_done, count(S, n, s + 1))
                    nc.gpsimd.tensor_tensor(hC[:, s % RC], hC[:, s % RC], hC[:, (s - 1) % RC], ALU.add
                                            ).then_inc(pair_added, 1)
                nc.gpsimd.tensor_copy(state[:, b, :, s:s + 1], h[:, r, :, T - 1:T]).then_inc(state_saved, 1)

            def back(s, m):
                if s == 0:
                    pool.wait_ge(y_skip, count(1, m, 1))
                    pool.wait_ge(sz_done, count(1, m, 1))
                    nc.gpsimd.tensor_tensor(yg[:, :, :], yg[:, :, :], sz[:, m[1]], ALU.mult).then_inc(yg_done, 1)
                if s == 3:
                    pool.wait_ge(xb_loaded, count(16, m, 16))
                    pool.wait_ge(x1_done, count(1, m, 1))
                    nc.gpsimd.tensor_tensor(xb[:, :, :], x1[:, :, :], xb[:, :, :], ALU.add).then_inc(x1x_done, 1)

            drive(pool, front, main, back, lambda s, m: None)

        @block.scalar
        def _(act):
            def load_xf(m):
                act.wait_ge(xn_done, count(1, m, 0))
                act.dma_start(xf[:, :, :], x_v[m[0], m[1]]).then_inc(xf_loaded, 16)

            load_xf((0, 0))
            act.wait_ge(loaded["par"], 16)
            act.wait_ge(consts_ready, 3)
            nc.scalar.preload_act_table_set("natural_log")
            nc.scalar.activation(ln_one[:, :], one_c[:, :], ACT.Ln).then_inc(ln_one_ready, 1)
            nc.scalar.preload_act_table_set("natural_log_exp_and_others")
            nc.scalar.activation(exp_a[:, :, :], par[:, C_ALOG:C_ALOG + NJ * S].rearrange("p (j s) -> p j s", s=S),
                                 ACT.Exp).then_inc(a_exp, 1)

            def inv_std(k, m):
                act.wait_ge(stats[k], count(1, m, 1))
                nc.scalar.activation(lnv[k][:, :], mv[k][:, :, 1], ACT.Ln, bias=eps_c[:, :]).then_inc(lnv_done[k], 1)
                act.wait_ge(lnv_done[k], count(1, m, 1))
                nc.scalar.activation(rstd[k][:, :], lnv[k][:, :], ACT.Exp, scale=-0.5).then_inc(rstd_done[k], 1)

            def use_log_exp():
                nc.scalar.preload_act_table_set("natural_log_exp_and_others")

            def front(s, m):
                b = m[1]
                if s == 0:
                    inv_std(0, m)
                if s == 1:
                    inv_std(1, m)
                if s == 2 and not is_last(m):
                    load_xf(following(m))
                if s == 3:
                    if is_first(m):
                        act.wait_ge(halo_zero, 1)
                    act.wait_ge(conv_tap, count(NJ * (TAPS - 1), m, -NJ * (TAPS - 1)))
                    nc.scalar.activation(xm[:, b, :, 0:TAPS - 1], xm[:, b, :, T:T + TAPS - 1], ACT.Copy
                                         ).then_inc(halo_moved, 1)
                    ps = front_bank("uT")
                    act.wait_ge(filled_f, front_use("uT", m))
                    nc.scalar.activation(uT[:, 0, :], ps[:, 0, :], ACT.Identity, scale=pcol(C_LN1W), bias=pcol(C_LN1B))
                    nc.scalar.activation(uT[:, 1, :], ps[:, 1, :], ACT.Identity, scale=pcol(C_LN1W + 1),
                                         bias=pcol(C_LN1B + 1)).then_inc(uT_done, 1)
                if s == 4:
                    act.wait_ge(halo_moved, count(1, m, 1))
                    act.wait_ge(sp_rest, count(1, m, 0))
                    for i in range(2):
                        ps = front_bank(f"x{i}")
                        act.wait_ge(filled_f, front_use(f"x{i}", m))
                        for k in range(2):
                            j = 2 * i + k
                            nc.scalar.activation(acc[:, j, :], ps[:, k, :], ACT.Identity,
                                                 scale=pcol(C_CONVW + j * TAPS + TAPS - 1), bias=pcol(C_CONVB + j)
                                                 ).then_inc(tap0_done, 1)
                        nc.scalar.activation(xm[:, b, 2 * i:2 * i + 2, TAPS - 1:], ps[:, :, :], ACT.Copy
                                             ).then_inc(xm_done, 1)
                if s == 7:
                    act.wait_ge(y_skip, count(1, m, -1))
                    act.wait_ge(conv_tap, count(NJ * (TAPS - 1), m, NJ * (TAPS - 1)))
                    nc.scalar.activation(xc[:, b, :, :], acc[:, :, :], ACT.Silu).then_inc(xc_done, 1)
                if s == 8 and is_first(m):
                    use_log_exp()
                if s == 9:
                    ps = front_bank("low")
                    act.wait_ge(filled_f, front_use("low", m))
                    nc.scalar.activation(low[:, :], ps[:, 0, :], ACT.Copy).then_inc(low_done, 1)
                if s == 10:
                    ps = front_bank("bc")
                    act.wait_ge(filled_f, front_use("bc", m))
                    act.wait_ge(bc_stored, count(16, m, 0))
                    nc.scalar.activation(bc[:, :], ps[0:2 * S, 0, :], ACT.Copy).then_inc(bc_done, 1)
                if s in (10, 11):
                    i = s - 10
                    act.wait_ge(scan_done, count(S, m, -S))
                    act.wait_ge(sp_added, count(1, m, 0))
                    ps = front_bank(f"dt{i}")
                    act.wait_ge(filled_f, front_use(f"dt{i}", m))
                    for k in range(2):
                        j = 2 * i + k
                        nc.scalar.activation(sp_e[:, j, :], ps[:, k, :], ACT.Abs, bias=pcol(C_DTB + j))
                        last = nc.scalar.activation(dt[:, b, j, :], ps[:, k, :], ACT.Relu, bias=pcol(C_DTB + j))
                    last.then_inc(relu_done, 1)
                if s == 11:
                    act.wait_ge(relu_done, count(2, m, 2))
                    nc.scalar.activation(sp_e[:, :, :], sp_e[:, :, :], ACT.Exp, scale=-1.0).then_inc(sp_exp, 1)
                if s == 15:
                    act.wait_ge(dt_done, count(1, m, 1))
                    if is_first(m):
                        act.wait_ge(a_ready, 1)
                    decay(0, m)
                if s in (14, 15):
                    i = s - 14
                    ps = front_bank(f"z{i}")
                    act.wait_ge(filled_f, front_use(f"z{i}", m))
                    act.wait_ge(yg_done, count(1, m, -1))
                    nc.scalar.activation(sz[:, b, 2 * i:2 * i + 2, :], ps[:, :, :], ACT.Copy).then_inc(z_copied, 1)
                if s == 11:
                    nc.scalar.preload_act_table_set("natural_log")
                    act.wait_ge(sp_exp, count(1, m, 1))
                    act.wait_ge(dt_done, count(1, m, 0))
                    nc.scalar.activation(sp_l[:, :, :], sp_e[:, :, :], ACT.Ln, bias=one_c[:, :]).then_inc(sp_ln, 1)
                    use_log_exp()

            def decay(s, n):
                act.wait_ge(scan_done, count(S, n, s + 1 - RA))
                for j in range(NJ):
                    last = nc.scalar.activation(dA[:, s % RA, j, :], dt[:, n[1], j, :], ACT.Exp,
                                                scale=neg_a[:, j, s:s + 1])
                last.then_inc(exp_done, 1)

            def main(s, n):
                if s == 8:
                    act.wait_ge(z_copied, count(2, n, 2))
                    nc.scalar.activation(sz[:, n[1]], sz[:, n[1]], ACT.Silu).then_inc(sz_done, 1)
                    use_log_exp()
                for k in range(1, AHEAD + 1) if s == 0 else (s + AHEAD,):
                    if k < S:
                        decay(k, n)

            def back(s, m):
                if s == 0:
                    act.wait_ge(x2_done, count(1, m, 0))
                    act.dma_start(xb[:, :, :], x_v[m[0], m[1]]).then_inc(xb_loaded, 16)
                    act.wait_ge(x1x_done, count(1, m, 0))
                    nc.scalar.activation(x1[:, :, :], xn[:, m[1]], ACT.Copy).then_inc(xn_copied, 1)
                if s == 3:
                    inv_std(2, m)
                if s == 4:
                    ps = back_bank("vT")
                    act.wait_ge(filled_b, back_use("vT", m))
                    nc.scalar.activation(nT[:, 0, :], ps[:, 0, :], ACT.Identity, scale=pcol(C_LN2W), bias=pcol(C_LN2B))
                    nc.scalar.activation(nT[:, 1, :], ps[:, 1, :], ACT.Identity, scale=pcol(C_LN2W + 1),
                                         bias=pcol(C_LN2B + 1)).then_inc(vT_done, 1)
                if s == 7:
                    act.wait_ge(filled_b, back_use_before("fo", m))
                    for i in range(2):
                        ps = back_bank(f"G{i}")
                        act.wait_ge(filled_b, back_use(f"G{i}", m))
                        nc.scalar.activation(hg[:, 2 * i:2 * i + 2, :], ps[:, :, :], ACT.Silu).then_inc(gate_done, 1)
                if s == 8 and is_last(m):
                    use_log_exp()
                if s == 10:
                    inv_std(3, m)
                if s == 11:
                    act.wait_ge(nrm_done, count(1, m, 1))
                    nc.scalar.activation(lnn[:, :], nrm[:, 2, :], ACT.Ln, scale=float(2 ** LIFT)).then_inc(lnn_done, 1)
                    act.wait_ge(lnn_done, count(1, m, 1))
                    nc.scalar.activation(rn[:, :], lnn[:, :], ACT.Exp, scale=-0.5, bias=lift_c[:, :]).then_inc(rn_done, 1)
                    ps = back_bank("xeT")
                    act.wait_ge(filled_b, back_use("xeT", m))
                    nc.scalar.activation(nT[:, :, :], ps[:, :, :], ACT.Copy).then_inc(xeT_done, 1)
                if s == 12:
                    act.wait_ge(lgm_done, count(1, m, 1))
                    nc.scalar.activation(pr[:, :, :], lgm[:, :, :], ACT.Exp).then_inc(pr_done, 1)
                if s == 13:
                    ps = back_bank("cT")
                    act.wait_ge(filled_b, back_use("cT", m))
                    act.wait_ge(cw_stored, count(16, m, 0))
                    nc.scalar.activation(cT[:, :], ps[0:NE].rearrange("p k t -> p (k t)")[:, 0:T], ACT.Copy
                                         ).then_inc(cT_done, 1)

            drive(act, front, main, back, lambda s, m: None)

        @block.vector
        def _(dve):
            nc.vector.memset(eps_c[:, :], EPS).then_inc(consts_ready, 1)
            nc.vector.memset(lift_c[:, :], 0.5 * LIFT * math.log(2.0)).then_inc(consts_ready, 1)
            nc.vector.memset(one_c[:, :], 1.0).then_inc(consts_ready, 1)
            dve.wait_ge(loaded["par"], 16)
            dve.wait_ge(ln_one_ready, 1)
            dve.wait_ge(a_exp, 1)
            nc.vector.tensor_scalar(neg_a[:, :, :], exp_a[:, :, :], -1.0, None, ALU.mult).then_inc(a_ready, 1)
            dve.wait_ge(state_zero, 1)

            links = {"f": 0, "b": 0}

            def link(which, m, ins):
                chain, per = (front_chain, LINKS_FRONT) if which == "f" else (back_chain, LINKS_BACK)
                links[which] = links[which] % per + 1
                ins.then_inc(chain, 1)
                dve.wait_ge(chain, count(per, m, links[which]))

            def norm_stats(k, src, which, m):
                for j in range(SUB):
                    last = nc.vector.bn_stats(bn[k][:, j, :], src[:, j, :])
                link(which, m, last)
                nc.vector.memset(pause[:, :], 0.0)
                for j in range(SUB):
                    last = nc.vector.bn_aggr(mv[k][:, j, :], bn[k][:, j, :])
                last.then_inc(stats[k], 1)

            def normalise(k, dst, src, done, m):
                dve.wait_ge(rstd_done[k], count(1, m, 1))
                for j in range(SUB):
                    last = nc.vector.tensor_scalar(dst[:, j, :], src[:, j, :], mv[k][:, j, 0:1], rstd[k][:, j:j + 1],
                                                   ALU.subtract, ALU.mult)
                last.then_inc(done, 1)

            def conv_at(tap, j):
                return 2 * NJ + j if tap == 3 else (j // 2) * 4 + (tap - 1) * 2 + j % 2

            def front(s, m):
                b = m[1]
                if s == 0:
                    dve.wait_ge(xf_loaded, count(16, m, 16))
                    norm_stats(0, xf, "f", m)
                if s == 1:
                    dve.wait_ge(xn_copied, count(1, m, -1))
                    normalise(0, xn[:, b], xf, xn_done, m)
                    dve.wait_ge(xn_done, count(1, m, 1))
                    norm_stats(1, xn[:, b], "f", m)
                if s == 2:
                    dve.wait_ge(filled_f, front_use_before("uT", m))
                    normalise(1, un, xn[:, b], un_done, m)
                if s in (CONV, CONV + 1):
                    for i in range(2):
                        if s == CONV:
                            dve.wait_ge(xm_done, count(2, m, i + 1))
                            dve.wait_ge(tap0_done, count(NJ, m, 2 * (i + 1)))
                        for tap in (1, 2) if s == CONV else (3,):
                            k = TAPS - 1 - tap
                            for j in (2 * i, 2 * i + 1):
                                if tap > 1:
                                    dve.wait_ge(conv_tap, count(NJ * (TAPS - 1), m, conv_at(tap - 1, j) + 1))
                                nc.vector.scalar_tensor_tensor(out=acc[:, j, :], in0=xm[:, b, j, k:k + T],
                                                               scalar=pcol(C_CONVW + j * TAPS + k), in1=acc[:, j, :],
                                                               op0=ALU.mult, op1=ALU.add).then_inc(conv_tap, 1)
                if s == SP_SLOT:
                    dve.wait_ge(sp_exp, count(1, m, 1))
                    dve.wait_ge(xc_done, count(1, m, 1))
                    nc.vector.tensor_scalar(acc[:, :, :], sp_e[:, :, :], 1.0, -1.0, ALU.add, ALU.add
                                            ).then_inc(sp_back, 1)
                if s == DT_SLOT:
                    dve.wait_ge(sp_ln, count(1, m, 1))
                    dve.wait_ge(sp_added, count(1, m, 1))
                    nc.vector.scalar_tensor_tensor(out=dt[:, b], in0=sp_l[:, :, :], scalar=ln_one[:, :],
                                                   in1=dt[:, b], op0=ALU.subtract, op1=ALU.add).then_inc(dt_done, 1)
                if s == 15:
                    dve.wait_ge(u_done, count(1, m, 1))
                    product(0, m)

            def product(s, n):
                b, r, g = n[1], s % RB, s // G
                dve.wait_ge(b_loaded[g % RINGG], count(16 * NG // RINGG, n, 16 * (g // RINGG + 1)))
                dve.wait_ge(scan_done, count(S, n, s + 1 - RB))
                nc.vector.tensor_tensor(bx[:, r], u[:, b],
                                        bB[:, g % RINGG, s % G:s % G + 1, :].to_broadcast([P, NJ, T]),
                                        ALU.mult).then_inc(bx_done["dve"], 1)

            def main(s, n):
                b, r = n[1], s % RB
                if s + 1 < S and s + 1 not in POOL_PRODUCTS:
                    product(s + 1, n)
                maker = "pool" if s in POOL_PRODUCTS else "dve"
                dve.wait_ge(bx_done[maker], products_done(maker, n, s + 1))
                dve.wait_ge(exp_done, count(S, n, s + 1))
                dve.wait_ge(hc_done, count(S, n, s + 1 - RB))
                dve.wait_ge(state_saved, count(S, n, s + 1 - RB))
                for j in range(NJ):
                    last = nc.vector.tensor_tensor_scan(h[:, r, j, :], dA[:, s % RA, j, :], bx[:, r, j, :],
                                                        state[:, b, j, s:s + 1], ALU.mult, ALU.add)
                last.then_inc(scan_done, 1)

            def weigh(i, m):
                ps = back_bank(f"wa{i}")
                dve.wait_ge(filled_b, back_use(f"wa{i}", m))
                if i == 0:
                    dve.wait_ge(cbc_loaded, count(16, m, 16))
                nc.vector.tensor_tensor(cbc[:, 2 * i:2 * i + 2, :], cbc[:, 2 * i:2 * i + 2, :], ps[:, :, :],
                                        ALU.mult).then_inc(hE_done, 1)

            def tail(s, m):
                if s in WEIGH:
                    for i in WEIGH[s]:
                        weigh(i, m)
                if s == FIN_SLOT:
                    dve.wait_ge(wb_filled, count(1, m, 1))
                    nc.vector.tensor_tensor(x2[:, :, :], x2[:, :, :], psb[WB_BANK][:, :, :], ALU.add
                                            ).then_inc(fin_done, 1)

            def back(s, m):
                b = m[1]
                if s == 0:
                    dve.wait_ge(y_summed, sums_done(m, S))
                    dve.wait_ge(filled_b, back_use_before("op", m))
                    for j in range(NJ):
                        last = nc.vector.scalar_tensor_tensor(out=yg[:, j, :], in0=xc[:, b, j, :],
                                                              scalar=pcol(C_DSKIP + j), in1=psy[j // 2][:, j % 2, :],
                                                              op0=ALU.mult, op1=ALU.add)
                    last.then_inc(y_skip, 1)
                if s == 3:
                    ps = back_bank("op")
                    dve.wait_ge(filled_b, back_use("op", m))
                    dve.wait_ge(xn_copied, count(1, m, 1))
                    nc.vector.tensor_tensor(x1[:, :, :], x1[:, :, :], ps[:, :, :], ALU.add).then_inc(x1_done, 1)
                    dve.wait_ge(x1_done, count(1, m, 1))
                    norm_stats(2, x1, "b", m)
                if s == 4:
                    dve.wait_ge(filled_b, back_use_before("xeT", m))
                    normalise(2, nx, x1, vn_done, m)
                if s == 8:
                    for i in range(2):
                        dve.wait_ge(gate_done, count(2, m, i + 1))
                        ps = back_bank(f"A{i}")
                        dve.wait_ge(filled_b, back_use(f"A{i}", m))
                        nc.vector.tensor_tensor(hg[:, 2 * i:2 * i + 2, :], hg[:, 2 * i:2 * i + 2, :], ps[:, :, :],
                                                ALU.mult).then_inc(hg_done, 1)
                if s == 10:
                    ps = back_bank("fo")
                    dve.wait_ge(filled_b, back_use("fo", m))
                    dve.wait_ge(x1x_done, count(1, m, 1))
                    dve.wait_ge(out_stored, count(16, m, 0))
                    nc.vector.tensor_tensor(x2[:, :, :], xb[:, :, :], ps[:, :, :], ALU.add).then_inc(x2_done, 1)
                    dve.wait_ge(x2_done, count(1, m, 1))
                    norm_stats(3, x2, "b", m)
                if s == 11:
                    normalise(3, nx, x2, xe_done, m)
                    var = mv[3][:, :, 1]
                    link("b", m, nc.vector.scalar_tensor_tensor(out=nrm[:, 0, :], in0=var, scalar=float(DM),
                                                                in1=rstd[3][:, :], op0=ALU.mult, op1=ALU.mult))
                    link("b", m, nc.vector.tensor_tensor(nrm[:, 1, :], nrm[:, 0, :], rstd[3][:, :], ALU.mult))
                    nc.vector.tensor_scalar(nrm[:, 2, :], nrm[:, 1, :], NORM_FLOOR * NORM_FLOOR, None, ALU.max
                                            ).then_inc(nrm_done, 1)
                if s == 12:
                    ps = back_bank("rt")
                    dve.wait_ge(filled_b, back_use("rt", m))
                    dve.wait_ge(rn_done, count(1, m, 1))
                    for j in range(SUB):
                        last = nc.vector.tensor_scalar(lg[:, j, :], ps[:, 0, j * NE:(j + 1) * NE], rn[:, j:j + 1], None,
                                                       ALU.mult)
                    link("b", m, last)
                    link("b", m, nc.vector.reduce_max(mx[:, :], lg[:, :, :], X))
                    nc.vector.tensor_tensor(lgm[:, :, :], lg[:, :, :], mx[:, :].unsqueeze(2).to_broadcast([P, SUB, NE]),
                                            ALU.subtract).then_inc(lgm_done, 1)
                if s == 13:
                    dve.wait_ge(pr_done, count(1, m, 1))
                    p_j = pr[:, :, :].unsqueeze(2).to_broadcast([P, SUB, NE, NE])
                    p_e = pr[:, :, :].unsqueeze(3).to_broadcast([P, SUB, NE, NE])
                    nc.vector.tensor_tensor(gt[:, :, :, :], p_j, p_e, ALU.is_gt)
                    link("b", m, nc.vector.tensor_tensor(eq[:, :, :, :], p_j, p_e, ALU.is_equal))
                    if is_first(m):
                        dve.wait_ge(earlier_ready, 1)
                    link("b", m, nc.vector.tensor_tensor(eq[:, :, :, :], eq[:, :, :, :],
                                                         earlier[:, :, :].unsqueeze(1).to_broadcast([P, SUB, NE, NE]),
                                                         ALU.mult))
                    link("b", m, nc.vector.tensor_tensor(gt[:, :, :, :], gt[:, :, :, :], eq[:, :, :, :], ALU.add))
                    link("b", m, nc.vector.reduce_sum(rank[:, :, :], gt[:, :, :, :], X))
                    link("b", m, nc.vector.scalar_tensor_tensor(out=psel[:, :, :], in0=rank[:, :, :], scalar=1.5,
                                                                in1=pr[:, :, :], op0=ALU.is_lt, op1=ALU.mult))
                    link("b", m, nc.vector.reduce_sum(den[:, :], psel[:, :, :], X))
                    link("b", m, nc.vector.reciprocal(rden[:, :], den[:, :]))
                    dve.wait_ge(filled_b, back_use_before("cT", m))
                    nc.vector.tensor_tensor(cw[:, :, :], psel[:, :, :], rden[:, :].unsqueeze(2).to_broadcast([P, SUB, NE]),
                                            ALU.mult).then_inc(cw_done, 1)
            drive(dve, front, main, back, tail)

        @block.tensor
        def _(pe):
            mm = nc.tensor.matmul
            pe.wait_ge(ident_ready, 1)

            def transposes(dst, src):
                for k in range(KM):
                    for j in range(SUB):
                        last = nc.tensor.transpose(dst[:, k, j * P:(j + 1) * P], src[:, j, k * P:(k + 1) * P], ident[:, :])
                return last

            def project(dst, w, rhs, kt, cols):
                for i, c in enumerate(cols):
                    for k in range(kt):
                        last = mm(dst[:, i, :], w[:, k, c:c + P], rhs[:, k, :], start=k == 0, stop=k == kt - 1)
                return last

            def project_tokens(dst, lhs, w, kt, halves=range(SUB)):
                for j in halves:
                    for k in range(kt):
                        last = mm(dst[:, j, :], lhs[:, k, j * P:(j + 1) * P], w[:, k, :], start=k == 0, stop=k == kt - 1)
                return last

            def first(m, key):
                if is_first(m):
                    pe.wait_ge(loaded[key], 16)

            def front(s, m):
                b = m[1]
                if s == 3:
                    ps = front_bank("uT")
                    pe.wait_ge(relu_done, count(2, m, 0))
                    pe.wait_ge(un_done, count(1, m, 1))
                    transposes(ps, un).then_inc(filled_f, 1)
                if s == 4:
                    first(m, "in")
                    pe.wait_ge(z_copied, count(2, m, 0))
                    pe.wait_ge(uT_done, count(1, m, 1))
                    for i in range(2):
                        project(front_bank(f"x{i}"), w_in_sb, uT, KM, [(2 * i + k) * P for k in range(2)]
                                ).then_inc(filled_f, 1)
                if s == 9:
                    first(m, "x")
                    pe.wait_ge(xc_done, count(1, m, 1))
                    for k in range(NJ):
                        last = mm(front_bank("low")[:, 0, :], w_x_sb[:, k, 0:DTR], xc[:, b, k, :],
                                  start=k == 0, stop=k == NJ - 1)
                    last.then_inc(filled_f, 1)
                    pe.wait_ge(xm_done, count(2, m, 1))
                    for k in range(NJ):
                        last = mm(front_bank("bc")[0:2 * S, 0, :], w_x_sb[:, k, DTR:DTR + 2 * S], xc[:, b, k, :],
                                  start=k == 0, stop=k == NJ - 1)
                    last.then_inc(filled_f, 1)
                    first(m, "dt")
                    pe.wait_ge(xm_done, count(2, m, 2))
                    pe.wait_ge(low_done, count(1, m, 1))
                    for i in range(2):
                        for k in range(2):
                            j = 2 * i + k
                            last = mm(front_bank(f"dt{i}")[:, k, :], w_dt_sb[:, j * P:(j + 1) * P], low[:, :],
                                      start=True, stop=True)
                        last.then_inc(filled_f, 1)
                if s == 13:
                    pe.wait_ge(bc_done, count(1, m, 1))
                    project(front_bank("z0"), w_in_sb, uT, KM, [DI, DI + P]).then_inc(filled_f, 1)
                if s == 14:
                    pe.wait_ge(relu_done, count(2, m, 1))
                    project(front_bank("z1"), w_in_sb, uT, KM, [DI + 2 * P, DI + 3 * P]).then_inc(filled_f, 1)

            def sum_slot(k):
                return min(k + 2 if k - 1 in ADDED else k + 1, S - 1)

            def sum_states(s, n):
                r = s % RC
                if s in ADDED:
                    return
                if s - 1 in ADDED:
                    pe.wait_ge(pair_added, count(len(ADDED), n, ADDED.index(s - 1) + 1))
                else:
                    pe.wait_ge(hc_done, count(S, n, s + 1))
                if s == 0:
                    pe.wait_ge(y_skip, count(1, n, 0))
                for i in range(2):
                    last = mm(psy[i][:, :, :], ident[:, :], hC[:, r, 2 * i:2 * i + 2, :], start=s == 0, stop=s == S - 1)
                last.then_inc(y_summed, 1)

            def main(s, n):
                for k in range(S):
                    if sum_slot(k) == s:
                        sum_states(k, n)

            def back(s, m):
                if s == 1:
                    first(m, "out")
                    pe.wait_ge(cT_done, count(1, m, 0))
                    pe.wait_ge(yg_done, count(1, m, 1))
                    project_tokens(back_bank("op"), yg, w_out_sb, NJ).then_inc(filled_b, 1)
                if s == 4:
                    pe.wait_ge(hE_done, count(NE // 2, m, -1))
                    pe.wait_ge(vn_done, count(1, m, 1))
                    transposes(back_bank("vT"), nx).then_inc(filled_b, 1)
                if s == 5:
                    first(m, "ff")
                    pe.wait_ge(x1_done, count(1, m, 1))
                    pe.wait_ge(vT_done, count(1, m, 1))
                    project(back_bank("G0"), w_ff_sb, nT, KM, [HID // 2, HID // 2 + P]).then_inc(filled_b, 1)
                if s == 6:
                    project(back_bank("G1"), w_ff_sb, nT, KM, [HID // 2 + 2 * P, HID // 2 + 3 * P]).then_inc(filled_b, 1)
                    pe.wait_ge(fin_done, count(1, m, 0))
                    project(back_bank("A0"), w_ff_sb, nT, KM, [0, P]).then_inc(filled_b, 1)
                if s == 7:
                    pe.wait_ge(gate_done, count(2, m, 1))
                    project(back_bank("A1"), w_ff_sb, nT, KM, [2 * P, 3 * P]).then_inc(filled_b, 1)
                if s == 8:
                    first(m, "fo")
                    pe.wait_ge(gate_done, count(2, m, 2))
                    pe.wait_ge(hg_done, count(2, m, 2))
                    project_tokens(back_bank("fo"), hg, w_fo_sb, F1).then_inc(filled_b, 1)
                if s == 11:
                    pe.wait_ge(xe_done, count(1, m, 1))
                    transposes(back_bank("xeT"), nx).then_inc(filled_b, 1)
                    first(m, "r")
                    pe.wait_ge(xeT_done, count(1, m, 1))
                    ps = back_bank("rt")
                    for j in range(SUB):
                        for k in range(KM):
                            last = mm(ps[:, 0, j * NE:(j + 1) * NE], nT[:, k, j * P:(j + 1) * P], w_r_sb[:, k, :],
                                      start=k == 0, stop=k == KM - 1)
                    last.then_inc(filled_b, 1)
                if s == 12:
                    first(m, "a")
                    pe.wait_ge(x2_done, count(1, m, 1))
                    low_rank(0, m)
                if s == 13:
                    low_rank(1, m)
                    pe.wait_ge(cw_done, count(1, m, 1))
                    ps = back_bank("cT")
                    for j in range(SUB):
                        last = nc.tensor.transpose(ps[0:NE, 0, j * P:(j + 1) * P], cw[:, j, :], ident[:, :])
                    last.then_inc(filled_b, 1)
            def low_rank(i, m):
                project(back_bank(f"wa{i}"), w_a_sb, nT, KM, [2 * i * RANK, (2 * i + 1) * RANK]).then_inc(filled_b, 1)

            def tail(s, m):
                if s == 0:
                    pe.wait_ge(hE_done, count(NE // 2, m, 1))
                    low_rank(2, m)
                    pe.wait_ge(hE_done, count(NE // 2, m, 2))
                    low_rank(3, m)
                if s == WB_SLOTS[0]:
                    first(m, "b")
                    pe.wait_ge(hE_done, count(NE // 2, m, NE // 2))
                    project_tokens(psb[WB_BANK], cbc, w_b_sb, NE, [0])
                if s == WB_SLOTS[1]:
                    project_tokens(psb[WB_BANK], cbc, w_b_sb, NE, [1]).then_inc(wb_filled, 1)

            drive(pe, front, main, back, tail)


def kernel(**inputs):
    import numpy as np
    import concourse.bacc as bacc
    from concourse.bass_utils import run_bass_kernel_spmd

    def get(name):
        return np.asarray(inputs[name])

    def tiles(w):
        k, m = w.shape
        return np.ascontiguousarray(w.reshape(k // P, P, m).transpose(1, 0, 2).reshape(P, -1))

    def columns(v):
        return tiles(v.reshape(v.shape[0], -1))

    params = np.ascontiguousarray(np.concatenate([
        columns(get("L0_attn_conv_w")), columns(get("L0_attn_conv_b")), columns(get("L0_attn_dt_proj_b")),
        columns(get("L0_attn_D_skip")), columns(get("L0_attn_A_log")),
        columns(get("L0_attn_ln1_w")), columns(get("L0_attn_ln1_b")),
        columns(get("L0_attn_ln2_w")), columns(get("L0_attn_ln2_b"))], axis=1))
    arrays = {
        "x": np.ascontiguousarray(get("L0_attn_x")),
        "params": params,
        "w_in": tiles(get("L0_attn_in_proj_w").T),
        "w_x": tiles(get("L0_attn_x_proj_w").T),
        "w_dt": tiles(get("L0_attn_dt_proj_w").T),
        "w_out": tiles(get("L0_attn_out_proj_w").T),
        "w_ff": tiles(get("L0_attn_ff_proj_w").T),
        "w_fo": tiles(get("L0_attn_ff_out_w").T),
        "w_a": tiles(get("L0_ffn_Wa").transpose(1, 0, 2).reshape(DM, NE * RANK)),
        "w_b": tiles(get("L0_ffn_Wb").reshape(NE * RANK, DM)),
        "w_r": tiles(get("L0_ffn_router_w")),
    }
    f32 = mybir.dt.float32
    nc = bacc.Bacc("TRN2", target_bir_lowering=False, num_devices=1)
    aps = {k: nc.dram_tensor(f"in_{k}", a.shape, f32, kind="ExternalInput").ap() for k, a in arrays.items()}
    bc_scratch = nc.dram_tensor("bc_scratch", (2 * S, T), f32, kind="Internal").ap()
    cw_scratch = nc.dram_tensor("cw_scratch", (NE, T), f32, kind="Internal").ap()
    out = nc.dram_tensor("out_0", (B, L, DM), f32, kind="ExternalOutput").ap()
    mamba_moe(nc, aps["x"], aps["params"], aps["w_in"], aps["w_x"], aps["w_dt"], aps["w_out"], aps["w_ff"],
              aps["w_fo"], aps["w_a"], aps["w_b"], aps["w_r"], bc_scratch, cw_scratch, out)
    r = run_bass_kernel_spmd(nc, [{f"in_{k}": a for k, a in arrays.items()}], core_ids=[0])
    return r.results[0]["out_0"]
```
